# Optimizing a Trainium2 kernel written in Bass

```python
import numpy as np
import jax
import jax.numpy as jnp

def _softmax(x, axis=-1):
    return jax.nn.softmax(x, axis=axis)

def _gelu(x):
    return jax.nn.gelu(x, approximate=True)

def _silu(x):
    return jax.nn.silu(x)

def _sigmoid(x):
    return jax.nn.sigmoid(x)

def _layernorm(x, axis=-1, eps=1e-05):
    m = jnp.mean(x, axis=axis, keepdims=True)
    v = jnp.var(x, axis=axis, keepdims=True)
    return (x - m) / jnp.sqrt(v + eps)

def _scatter_add(tgt, idx, src, axis=0):
    return tgt.at[idx].add(src)

def _segment_sum(src, seg, n):
    return jax.ops.segment_sum(src, seg, n)
kernel_name = 'mk_gnn_preln_d4_gnn_r8_78c9fd'

def setup_inputs(seed: int=0):
    np.random.seed(seed)
    _w = jnp.asarray

    def _rec_inputs():
        import jax
        import jax.numpy as jnp
        _gk = jax.random.key(seed)
        x = -0.000202 + 1 * jax.random.normal(jax.random.fold_in(_gk, 1), (6250, 64), jnp.float32)
        _s = jax.random.randint(jax.random.fold_in(_gk, 2), (100000,), 0, 6250, jnp.int32)
        _d = jax.random.randint(jax.random.fold_in(_gk, 3), (100000,), 0, 6250, jnp.int32)
        _loop = jnp.arange(6250, dtype=jnp.int32)
        src = jnp.concatenate([_s, _d, _loop])
        dst = jnp.concatenate([_d, _s, _loop])
        _o = jnp.argsort(dst, stable=True)
        src = src[_o]
        dst = dst[_o]
        edge_type_16 = jax.random.randint(jax.random.fold_in(_gk, 13), (206250,), 0, 16, jnp.int32)
        edge_type_32 = jax.random.randint(jax.random.fold_in(_gk, 14), (206250,), 0, 32, jnp.int32)
        edge_weight = 9.9816e-05 + 0.999782 * jax.random.normal(jax.random.fold_in(_gk, 15), (206250,), jnp.float32)
        return (x, src, dst, edge_type_16, edge_type_32, edge_weight)
    x, src, dst, edge_type_16, edge_type_32, edge_weight = _rec_inputs()

    def _L0_gnn_setup():
        import jax, jax.numpy as jnp
        import numpy as np
        N_NODES = 12500
        N_EDGES = 156250
        D_FEAT = 64

        def _segment_softmax(vals, idx, num_segments):
            seg_max = jax.ops.segment_max(vals, idx, num_segments=num_segments)
            e = jnp.exp(vals - seg_max[idx])
            seg_sum = jax.ops.segment_sum(e, idx, num_segments=num_segments)
            return e / seg_sum[idx]
        key = jax.random.key(seed)
        k1, k2, k3 = jax.random.split(key, 3)
        x = jax.random.normal(k1, (N_NODES, D_FEAT), dtype=jnp.float32)
        edge_index = jax.random.randint(k2, (2, N_EDGES), 0, N_NODES, dtype=jnp.int32)
        edge_attrs = jax.random.normal(k3, (N_EDGES,), dtype=jnp.float32)
        return {'x': x, 'edge_index': edge_index, 'edge_attrs': edge_attrs}
    _L0_gnn_all = _L0_gnn_setup()
    _L0_gnn_in = {k: v for k, v in _L0_gnn_all.items() if k in ()}
    del _L0_gnn_all

    def _L1_gnn_setup():
        import jax, jax.numpy as jnp
        import numpy as np
        N_NODES = 6250
        N_EDGES = 100000
        D_FEAT = 64
        N_LAYERS = 2
        EPS = 1e-12

        def _agnn_layer(h, src, dst, beta, n_nodes):
            norm = jnp.sqrt(jnp.sum(h * h, axis=-1, keepdims=True))
            nh = h / jnp.maximum(norm, EPS)
            cos = jnp.sum(nh[src] * nh[dst], axis=-1)
            e = beta * cos
            m = jax.ops.segment_max(e, dst, num_segments=n_nodes)
            ee = jnp.exp(e - m[dst])
            den = jax.ops.segment_sum(ee, dst, num_segments=n_nodes)
            p = ee / den[dst]
            out = jax.ops.segment_sum(h[src] * p[:, None], dst, num_segments=n_nodes)
            return jax.nn.relu(out)
        key = jax.random.key(seed)
        k1, k2, k3 = jax.random.split(key, 3)
        x = jax.random.normal(k1, (N_NODES, D_FEAT), dtype=jnp.float32)
        src = jax.random.randint(k2, (N_EDGES,), 0, N_NODES, dtype=jnp.int64)
        dst = jax.random.randint(k3, (N_EDGES,), 0, N_NODES, dtype=jnp.int64)
        beta = jnp.ones((N_LAYERS,), dtype=jnp.float32)
        return {'x': x, 'src': src, 'dst': dst, 'beta': beta}
    _L1_gnn_all = _L1_gnn_setup()
    _L1_gnn_in = {k: v for k, v in _L1_gnn_all.items() if k in ('beta',)}
    del _L1_gnn_all

    def _L2_gnn_setup():
        import jax, jax.numpy as jnp
        import numpy as np
        N_NODES = 12500
        N_EDGES = 125000
        D_IN = 64
        D_OUT = 64
        N_RELS = 16
        key = jax.random.key(seed)
        k1, k2, k3, k4, k5 = jax.random.split(key, 5)
        feat = jax.random.normal(k1, (N_NODES, D_IN), dtype=jnp.float32)
        weight = jax.random.normal(k2, (N_RELS, D_IN, D_OUT), dtype=jnp.float32) * 0.05
        src = jax.random.randint(k3, (N_EDGES,), 0, N_NODES)
        dst = jax.random.randint(k4, (N_EDGES,), 0, N_NODES)
        etypes = jax.random.randint(k5, (N_EDGES,), 0, N_RELS)
        return {'feat': feat, 'weight': weight, 'src': src, 'dst': dst, 'etypes': etypes}
    _L2_gnn_all = _L2_gnn_setup()
    _L2_gnn_in = {k: v for k, v in _L2_gnn_all.items() if k in ('weight',)}
    del _L2_gnn_all

    def _L3_gnn_setup():
        import jax, jax.numpy as jnp
        import numpy as np
        N_NODES = 12500
        N_EDGES = 125000
        IN_F = 64
        OUT_F = 64
        N_REL = 32
        N_BASES = 30
        key = jax.random.key(seed)
        k = jax.random.split(key, 8)
        node_features = jax.random.normal(k[0], (N_NODES, IN_F), dtype=jnp.float32)
        senders = jax.random.randint(k[1], (N_EDGES,), 0, N_NODES, dtype=jnp.int32)
        receivers = jax.random.randint(k[2], (N_EDGES,), 0, N_NODES, dtype=jnp.int32)
        relation_types = jax.random.randint(k[3], (N_EDGES,), 0, N_REL, dtype=jnp.int32)
        basis = jax.random.normal(k[4], (N_BASES, IN_F, OUT_F), dtype=jnp.float32) * 0.01
        coeff = jax.random.normal(k[5], (N_REL, N_BASES), dtype=jnp.float32) * 0.01
        self_weight = jax.random.normal(k[6], (IN_F, OUT_F), dtype=jnp.float32) * 0.01
        bias = jnp.zeros((OUT_F,), dtype=jnp.float32)
        return {'node_features': node_features, 'senders': senders, 'receivers': receivers, 'relation_types': relation_types, 'basis': basis, 'coeff': coeff, 'self_weight': self_weight, 'bias': bias}
    _L3_gnn_all = _L3_gnn_setup()
    _L3_gnn_in = {k: v for k, v in _L3_gnn_all.items() if k in ('basis', 'coeff', 'self_weight', 'bias')}
    del _L3_gnn_all
    return {'x': x, 'src': src, 'dst': dst, 'edge_type_16': edge_type_16, 'edge_type_32': edge_type_32, 'edge_weight': edge_weight, 'L1_gnn_beta': _L1_gnn_in['beta'], 'L2_gnn_weight': _L2_gnn_in['weight'], 'L3_gnn_basis': _L3_gnn_in['basis'], 'L3_gnn_coeff': _L3_gnn_in['coeff'], 'L3_gnn_self_weight': _L3_gnn_in['self_weight'], 'L3_gnn_bias': _L3_gnn_in['bias']}

def reference(x, src, dst, edge_type_16, edge_type_32, edge_weight, L1_gnn_beta, L2_gnn_weight, L3_gnn_basis, L3_gnn_coeff, L3_gnn_self_weight, L3_gnn_bias):
    import jax
    import jax.numpy as jnp

    def _L0_gnn_ref(x, edge_index, edge_attrs):
        import jax, jax.numpy as jnp
        import numpy as np
        N_NODES = 12500
        N_EDGES = 156250
        D_FEAT = 64

        def _segment_softmax(vals, idx, num_segments):
            seg_max = jax.ops.segment_max(vals, idx, num_segments=num_segments)
            e = jnp.exp(vals - seg_max[idx])
            seg_sum = jax.ops.segment_sum(e, idx, num_segments=num_segments)
            return e / seg_sum[idx]
        n = x.shape[0]
        from_, to_ = (edge_index[0], edge_index[1])
        incoming_norm = _segment_softmax(edge_attrs, to_, n)
        outgoing_norm = _segment_softmax(edge_attrs, from_, n)
        norm = jnp.sqrt(incoming_norm * outgoing_norm)
        messages = norm[:, None] * x[from_]
        return jax.ops.segment_sum(messages, to_, num_segments=n)

    def _L1_gnn_ref(x, src, dst, beta):
        import jax, jax.numpy as jnp
        import numpy as np
        N_NODES = 6250
        N_EDGES = 100000
        D_FEAT = 64
        N_LAYERS = 2
        EPS = 1e-12

        def _agnn_layer(h, src, dst, beta, n_nodes):
            norm = jnp.sqrt(jnp.sum(h * h, axis=-1, keepdims=True))
            nh = h / jnp.maximum(norm, EPS)
            cos = jnp.sum(nh[src] * nh[dst], axis=-1)
            e = beta * cos
            m = jax.ops.segment_max(e, dst, num_segments=n_nodes)
            ee = jnp.exp(e - m[dst])
            den = jax.ops.segment_sum(ee, dst, num_segments=n_nodes)
            p = ee / den[dst]
            out = jax.ops.segment_sum(h[src] * p[:, None], dst, num_segments=n_nodes)
            return jax.nn.relu(out)
        n_nodes = x.shape[0]
        h = x
        for i in range(beta.shape[0]):
            h = _agnn_layer(h, src, dst, beta[i], n_nodes)
        return h

    def _L2_gnn_ref(feat, weight, src, dst, etypes):
        import jax, jax.numpy as jnp
        import numpy as np
        N_NODES = 12500
        N_EDGES = 125000
        D_IN = 64
        D_OUT = 64
        N_RELS = 16
        h = feat[src]
        n_rels = weight.shape[0]
        e, d_out = (h.shape[0], weight.shape[2])

        def step(m, rw):
            r, w_r = rw
            mask = jnp.where(etypes == r, 1.0, 0.0).astype(h.dtype)
            m = m + mask[:, None] * (h @ w_r)
            return (m, None)
        m0 = jnp.zeros((e, d_out), dtype=h.dtype)
        m, _ = jax.lax.scan(step, m0, (jnp.arange(n_rels), weight))
        out = jax.ops.segment_sum(m, dst, num_segments=feat.shape[0])
        return out

    def _L3_gnn_ref(node_features, senders, receivers, relation_types, basis, coeff, self_weight, bias):
        import jax, jax.numpy as jnp
        import numpy as np
        N_NODES = 12500
        N_EDGES = 125000
        IN_F = 64
        OUT_F = 64
        N_REL = 32
        N_BASES = 30
        num_nodes = node_features.shape[0]
        n_edges = senders.shape[0]
        rel_weights = jnp.einsum('rb,bio->rio', coeff, basis)
        src_features = node_features[senders]
        seg_ids = receivers * N_REL + relation_types
        agg = jax.ops.segment_sum(src_features, seg_ids, num_segments=num_nodes * N_REL)
        agg = agg.reshape(num_nodes, N_REL, node_features.shape[1])
        aggregated = jnp.einsum('nri,rio->no', agg, rel_weights)
        ones = jnp.ones((n_edges,), dtype=node_features.dtype)
        in_degree = jax.ops.segment_sum(ones, receivers, num_segments=num_nodes)
        in_degree = jnp.maximum(in_degree, 1.0)
        out = aggregated / in_degree[:, None]
        out = out + node_features @ self_weight
        out = out + bias
        return out
    edge_index = jnp.stack([src, dst])
    h = jnp.maximum(_layernorm(x, axis=-1), 0.0)
    x = x + _L0_gnn_ref(h, edge_index, edge_weight)
    h = jnp.maximum(_layernorm(x, axis=-1), 0.0)
    x = x + _L1_gnn_ref(h, src, dst, L1_gnn_beta)
    h = jnp.maximum(_layernorm(x, axis=-1), 0.0)
    x = x + _L2_gnn_ref(h, L2_gnn_weight, src, dst, edge_type_16)
    h = jnp.maximum(_layernorm(x, axis=-1), 0.0)
    x = x + _L3_gnn_ref(h, src, dst, edge_type_32, L3_gnn_basis, L3_gnn_coeff, L3_gnn_self_weight, L3_gnn_bias)
    return x

_drawn_inputs = setup_inputs


def setup_inputs(seed=0):
    import zlib

    import numpy as np

    out = dict(_drawn_inputs(seed))
    spreads = {'L1_gnn_beta': (1.0, 0.6), 'L3_gnn_bias': (0.0, 0.1)}
    factors = {'L3_gnn_basis': 25.092, 'L3_gnn_coeff': 24.135}
    for name, (base, spread) in spreads.items():
        noise = np.random.default_rng([zlib.crc32(name.encode()), seed]).standard_normal(out[name].shape)
        drawn = base * np.exp(spread * noise) if base else spread * noise
        out[name] = jnp.asarray(drawn.astype(out[name].dtype))
    for name, factor in factors.items():
        out[name] = (out[name] * factor).astype(out[name].dtype)
    return out
```

```python
import concourse.bass as bass
from concourse import mybir
from contextlib import ExitStack

F32 = mybir.dt.float32
BF16 = mybir.dt.bfloat16
I32 = mybir.dt.int32
ALU = mybir.AluOpType
ACT = mybir.ActivationFunctionType
AX = mybir.AxisListType.X

P = 128
ITEMS = 4
RING = 4
CREDIT = 4
D = 64
ROW = D + 1
BIG = float(2 ** 100)
LN_EPS = 1e-5
NORM_EPS = 1e-12


class Plan:

    def __init__(self, nodes, edges, rel_a, rel_b, bases):
        self.nodes, self.edges = nodes, edges
        self.rel_a, self.rel_b, self.bases = rel_a, rel_b, bases
        self.blocks = -(-nodes // P)
        self.last = nodes - (self.blocks - 1) * P
        self.lanes = max(d for d in range(1, P + 1) if edges % d == 0)
        self.cols = edges // self.lanes
        self.stage = max(c for c in range(1, 21) if self.cols % (2 * c) == 0)
        self.stages = self.cols // (2 * self.stage)
        most = (edges + self.blocks * (ITEMS * P - 1)) // (ITEMS * P)
        self.groups = -(-most // 4) * 4
        self.items = self.groups * ITEMS


class At:

    def __init__(self, rnd, slot):
        self.rnd, self.slot, self.half = rnd, slot, slot % 2
        self.g = rnd * 4 + slot


def gnn_program(nc, x, src, dst, type_a, type_b, weight, beta, w_a, basis, coeff, w_self, bias, out):
    pl = Plan(x.shape[0], src.shape[0], w_a.shape[0], coeff.shape[0], basis.shape[0])
    NB, LANES, COLS, NI, NG = pl.blocks, pl.lanes, pl.cols, pl.items, pl.groups
    CH = pl.stage
    FULL = NB - 1 if pl.last < P else NB

    def scratch(name, shape, dt=F32):
        return nc.dram_tensor(name, shape, dt).ap()

    bins_dst = scratch("bins_dst", (P * NI, 5), I32)
    bins_src = scratch("bins_src", (P * NI, 2), I32)
    tables = [scratch(f"table{k}", (NB * P, ROW)) for k in range(3)]
    table_a = scratch("table_a", (NB * P * pl.rel_a, D))
    table_b = scratch("table_b", (NB * P * pl.rel_b, D))
    rel_w = scratch("rel_w", (pl.rel_b, D, D))

    ctx = ExitStack()
    with ctx:
        def sb(name, shape, dt=F32):
            return ctx.enter_context(nc.sbuf_tensor(name, shape, dt))

        def sem(name):
            return ctx.enter_context(nc.semaphore(name))

        ZW = max(8 * COLS, 2 * NB * D + NB * ROW + (RING + 2) * ITEMS * ROW)
        Z = sb("Z", [P, ZW])
        pay_d = sb("pay_d", [P, max(COLS * 6, NB * ROW + 3 * NB * D // 2 + D)], I32)
        pay_s = sb("pay_s", [P, max(COLS * 3, (pl.rel_a + pl.rel_b) * D)], I32)
        pd = sb("pd", [P, max(NI * 5, 2 * D * D)], I32)
        ps = sb("ps", [P, max(NI * 2, 4 * 512)], I32)

        def zcol(k, dt=F32):
            return Z[0:LANES, k * COLS:(k + 1) * COLS].bitcast(dt) if dt != F32 else Z[0:LANES, k * COLS:(k + 1) * COLS]

        src_c, dst_c, typ_c = zcol(0, I32), zcol(1, I32), zcol(2, I32)
        wgt_c, bin_c, pos_c, hot_c, run_c = zcol(3), zcol(4), zcol(5), zcol(6), zcol(7)
        hot_i, run_i, pos_i = zcol(6, I32), zcol(7, I32), zcol(5, I32)
        payd = pay_d[0:LANES, 0:COLS * 6].rearrange("p (c f) -> p c f", f=6)
        paydf = pay_d[0:LANES, 0:COLS * 6].bitcast(F32).rearrange("p (c f) -> p c f", f=6)
        pays = pay_s[0:LANES, 0:COLS * 3].rearrange("p (c f) -> p c f", f=3)
        paysf = pay_s[0:LANES, 0:COLS * 3].bitcast(F32).rearrange("p (c f) -> p c f", f=3)
        slot_d = sb("slot_d", [P, 2, CH, 6], I32)
        slot_s = sb("slot_s", [P, 2, CH, 3], I32)
        pdi = pd[:, 0:NI * 5].rearrange("p (n f) -> p n f", f=5)
        pdf = pd[:, 0:NI * 5].bitcast(F32).rearrange("p (n f) -> p n f", f=5)
        psf = ps[:, 0:NI * 2].bitcast(F32).rearrange("p (n f) -> p n f", f=2)
        basis_sb = pd[0:pl.bases, 0:D * D].bitcast(F32)
        relw_sb = pd[0:pl.rel_b, D * D:2 * D * D].bitcast(F32)
        o = 0
        x_sb = Z[:, o:o + NB * D].rearrange("p (b f) -> p b f", f=D)
        o += NB * D
        h_sb = Z[:, o:o + NB * D].rearrange("p (b f) -> p b f", f=D)
        o += NB * D
        tab_flat = Z[:, o:o + NB * ROW]
        tab = tab_flat.rearrange("p (b f) -> p b f", f=ROW)
        sq = Z[:, o:o + NB * D].rearrange("p (b f) -> p b f", f=D)
        o += NB * ROW
        rows = Z[:, o:o + RING * ITEMS * ROW].rearrange("p (s j f) -> p s j f", s=RING, j=ITEMS)
        o += RING * ITEMS * ROW
        msg = Z[:, o:o + 2 * ITEMS * ROW].rearrange("p (s j f) -> p s j f", s=2, j=ITEMS)
        acc = pay_d[:, 0:NB * ROW].bitcast(F32).rearrange("p (b f) -> p b f", f=ROW)
        unit3 = pay_d[:, NB * ROW:NB * ROW + 3 * NB * D // 2].bitcast(BF16).rearrange("p (k b f) -> p k b f", k=3, f=D)
        wa_sb = pay_s[0:D, 0:pl.rel_a * D].bitcast(F32)
        wb_sb = pay_s[0:D, pl.rel_a * D:(pl.rel_a + pl.rel_b) * D].bitcast(F32)
        stg = ps[:, 0:4 * 512].bitcast(F32).rearrange("p (s c) -> p s c", s=4)

        iota = sb("iota", [P, 512])
        lane = sb("lane", [P, 1])
        ident = sb("ident", [P, P])
        ident_b = sb("ident_b", [P, P], BF16)
        before = sb("before", [P, P])
        ones = sb("ones", [P, P])
        neg_big = sb("neg_big", [P, 1])
        tiny_zero = sb("tiny_zero", [P, 1])
        coeff_t = sb("coeff_t", [pl.bases, pl.rel_b])
        wself_sb = sb("wself_sb", [D, D])
        bias_sb = sb("bias_sb", [P, D])
        beta_sb = sb("beta_sb", [P, 2])
        lane_bin = sb("lane_bin", [P, NB])
        bin_groups = sb("bin_groups", [P, NB])
        bin_groups_i = sb("bin_groups_i", [P, NB], I32)
        bin_first = sb("bin_first", [P, NB])
        bin_zero = sb("bin_zero", [P, NB])
        bin_from = sb("bin_from", [P, NB])
        first_col = sb("first_col", [NB, 1])
        reached = sb("reached", [NB, NG])
        block_s = sb("block_s", [1, NG], I32)
        block_d = sb("block_d", [1, NG], I32)

        idx = sb("idx", [P, RING, ITEMS], I32)
        hot = sb("hot", [P, RING, ITEMS, P])
        hot_t = sb("hot_t", [P, RING, ITEMS, P], BF16)
        pen_t = sb("pen_t", [P, 2, ITEMS * P], BF16)
        score = sb("score", [P, 2, ITEMS])
        score_b = sb("score_b", [P, 2, ITEMS], BF16)
        prod = sb("prod", [P, 2, ITEMS, D])
        dot = sb("dot", [P, 2, ITEMS])
        gmax = sb("gmax", [P, 2])
        new_max = sb("new_max", [P, 2], BF16)
        drop = sb("drop", [P, 2])
        keep = sb("keep", [P, 2, 2])
        shifted = sb("shifted", [P, 2, 2, ITEMS])
        less_src = sb("less_src", [P, 2, ITEMS])
        expd = sb("expd", [P, 2, 2, ITEMS])
        run_max = sb("run_max", [P, NB])
        out_sum = sb("out_sum", [P, NB])
        col_a = sb("col_a", [P, NB])
        col_b = sb("col_b", [P, NB])
        col_c = sb("col_c", [P, NB])
        h_blk = sb("h_blk", [P, 2, P])
        ht = sb("ht", [D, 2, P])

        pbig = ctx.enter_context(nc.psum_tensor("pbig", [P, 4, 512], F32))
        p_t, p_v = pbig[:, 0:2, :], pbig[:, 2:4, :]
        prow = ctx.enter_context(nc.psum_tensor("prow", [P, 2, 512], F32))
        p_row = prow[:, :, 0:ITEMS * D].rearrange("p s (j f) -> p s j f", j=ITEMS)
        p_max = ctx.enter_context(nc.psum_tensor("p_max", [P, 512], F32))
        p_sum = ctx.enter_context(nc.psum_tensor("p_sum", [P, 512], F32))
        p_cnt, p_col, p_turn = prow[:, 0, :], prow[:, 1, :], prow[:, :, 0:P]

        loaded_ids, loaded_w, loaded_types = sem("loaded_ids"), sem("loaded_w"), sem("loaded_types")
        loaded_basis, loaded_small = sem("loaded_basis"), sem("loaded_small")
        iota_made, consts_made = sem("iota_made"), sem("consts_made")
        relw_made, relw_kept, relw_stored = sem("relw_made"), sem("relw_kept"), sem("relw_stored")
        pads_made, pads_stored = sem("pads_made"), sem("pads_stored")
        counted, offsets_made, first_made, first_col_made = sem("counted"), sem("offsets_made"), sem("first_made"), sem("first_col_made")
        first_col_kept, reached_made, block_made = sem("first_col_kept"), sem("reached_made"), sem("block_made")
        blocks_ready = sem("blocks_ready")
        types_used = sem("types_used")
        pay_ready = sem("pay_ready")
        staged = [sem("staged0"), sem("staged1")]
        scattered = [sem("scattered0"), sem("scattered1")]
        scatters_started = sem("scatters_started")
        bins_loaded_s, bins_loaded_d = sem("bins_loaded_s"), sem("bins_loaded_d")
        x_cleared, x_loaded = sem("x_cleared"), sem("x_loaded")
        dve_step = sem("dve_step")
        dve_asks_act, act_answers = sem("dve_asks_act"), sem("act_answers")
        table_made, table_stored = sem("table_made"), sem("table_stored")
        units_made, sums_cleared = sem("units_made"), sem("sums_cleared")
        weights_loaded, h_made, out_made, out_stored = sem("weights_loaded"), sem("h_made"), sem("out_made"), sem("out_stored")
        blk_copied, blk_turned, ht_kept = sem("blk_copied"), sem("blk_turned"), sem("ht_kept")
        self_made, self_added = sem("self_made"), sem("self_added")
        chunk_made = [sem(f"chunk_made{k}") for k in range(4)]
        chunk_kept = [sem(f"chunk_kept{k}") for k in range(4)]
        chunk_stored = [sem(f"chunk_stored{k}") for k in range(4)]
        idx_ready = sem("idx_ready")
        gathers_started = sem("gathers_started")
        gathered = [sem(f"gathered{s}") for s in range(RING)]
        hot_made, turned, hot_t_made, pen_made = sem("hot_made"), sem("turned"), sem("hot_t_made"), sem("pen_made")
        dst_rows, multiplied, dotted, scored, scored_b = sem("dst_rows"), sem("multiplied"), sem("dotted"), sem("scored"), sem("scored_b")
        spread, group_max, max_made, dropped, max_kept = sem("spread"), sem("group_max"), sem("max_made"), sem("dropped"), sem("max_kept")
        keep_made, edge_max, shift_made, exp_made = sem("keep_made"), sem("edge_max"), sem("shift_made"), sem("exp_made")
        unsourced = sem("unsourced")
        msg_made, summed, added = sem("msg_made"), sem("summed"), sem("added")

        def done(n):
            return n + 1 + CREDIT

        SOURCE, EDGE, AGNN, PLAIN = "source", "edge", "agnn", "plain"

        class Pass:
            def __init__(self, kind, every, gather, own, column=0, table=None):
                self.kind, self.column, self.table = kind, column, table
                self.every = every * NG
                self.gather = gather * NG
                self.rounds = gather * (NG // 4)
                self.own = own * NG
                self.softmax = kind != PLAIN
                self.block = block_s if kind == SOURCE else block_d
                self.local = psf[:, :, 0] if kind == SOURCE else pdf[:, :, 1]
                self.weight = psf[:, :, 1] if kind == SOURCE else pdf[:, :, 2]

        p_source = Pass(SOURCE, 0, 0, 0)
        p_edge = Pass(EDGE, 1, 0, 0, 0, tables[0])
        p_agnn = [Pass(AGNN, 2, 1, 0, 0, tables[1]), Pass(AGNN, 3, 2, 1, 0, tables[2])]
        p_plain = [Pass(PLAIN, 4, 3, 0, 3, table_a), Pass(PLAIN, 5, 4, 1, 4, table_b)]

        def run_pass(eng, ahead, middle, behind, late):
            def turn(before_, now, after):
                if after is not None:
                    ahead(after)
                if now is not None:
                    middle(now)
                if before_ is not None:
                    behind(before_)
                if now is not None:
                    late(now)

            turn(None, None, At(0, 0))
            turn(None, At(0, 0), At(0, 1))
            with eng.Fori(0, NG // 4 - 1) as t:
                for k in range(1, 5):
                    turn(At(t, k - 1), At(t + k // 4, k % 4), At(t + (k + 1) // 4, (k + 1) % 4))
            t = NG // 4 - 1
            turn(At(t, 0), At(t, 1), At(t, 2))
            turn(At(t, 1), At(t, 2), At(t, 3))
            turn(At(t, 2), At(t, 3), None)
            turn(At(t, 3), None, None)

        def nothing(at):
            pass

        PER = [pl.rel_a * D // 512, pl.rel_b * D // 512]
        CB = [[0] * PER[0], [NB * (c < PER[0]) for c in range(PER[1])]]

        def over_blocks(eng, one):
            with eng.Fori(0, NB // 2) as t:
                for half in range(2):
                    one(t * 2 + half, half)
            if NB % 2:
                one(NB - 1, (NB - 1) % 2)

        block = ctx.enter_context(nc.Block())

        @block.sync
        def _(sp):
            def lanes(a):
                return a.rearrange("(p c) -> p c", c=COLS)

            sp.dma_start(src_c, lanes(src)).then_inc(loaded_ids, 16)
            sp.dma_start(dst_c, lanes(dst)).then_inc(loaded_ids, 16)
            sp.dma_start(wgt_c, lanes(weight)).then_inc(loaded_w, 16)
            sp.dma_start(typ_c, lanes(type_a)).then_inc(loaded_types, 16)
            sp.dma_start(basis_sb, basis.rearrange("b i o -> b (i o)")).then_inc(loaded_basis, 16)
            sp.dma_start(coeff_t[:, :], coeff.rearrange("r b -> b r"), allow_slow_non_contiguous=True).then_inc(loaded_basis, 16)
            sp.dma_start(wself_sb[:, :], w_self).then_inc(loaded_small, 16)
            sp.dma_start(bias_sb[:, :], bias.unsqueeze(0).to_broadcast([P, D])).then_inc(loaded_small, 16)
            sp.dma_start(beta_sb[:, :], beta.unsqueeze(0).to_broadcast([P, 2])).then_inc(loaded_small, 16)
            sp.wait_ge(relw_kept, 8)
            sp.dma_start(rel_w.rearrange("r i o -> r (i o)"), relw_sb).then_inc(relw_stored, 16)
            sp.wait_ge(pads_made, 1)
            sp.dma_start(bins_src.rearrange("(p n) f -> p (n f)", p=P), ps[:, 0:NI * 2]).then_inc(pads_stored, 16)
            sp.wait_ge(pads_made, 2)
            sp.dma_start(bins_dst.rearrange("(p n) f -> p (n f)", p=P), pd[:, 0:NI * 5]).then_inc(pads_stored, 16)
            sp.wait_ge(types_used, 1)
            sp.dma_start(typ_c, lanes(type_b)).then_inc(loaded_types, 16)

            def stage(pay, slot, s, t, uses):
                sp.wait_ge(scattered[s], (t + uses) * (16 * CH))
                sp.dma_start(slot[0:LANES, s, :, :], pay[:, bass.ds((t * 2 + s) * CH, CH), :]).then_inc(staged[s], 16)

            sp.wait_ge(pay_ready, 1)
            with sp.Fori(0, pl.stages) as t:
                for s in range(2):
                    stage(pays, slot_s, s, t, 0)
            for s in range(2):
                sp.wait_ge(scattered[s], pl.stages * 16 * CH)
            sp.dma_start(ps[:, 0:NI * 2], bins_src.rearrange("(p n) f -> p (n f)", p=P)).then_inc(bins_loaded_s, 16)
            sp.wait_ge(pay_ready, 2)
            sp.wait_ge(x_cleared, 1)
            sp.dma_start(x_sb[:, 0:FULL, :], x[0:FULL * P, :].rearrange("(b p) f -> p b f", p=P)).then_inc(x_loaded, 16)
            if FULL < NB:
                sp.dma_start(x_sb[0:pl.last, FULL, :], x[FULL * P:, :]).then_inc(x_loaded, 16)
            sp.wait_ge(relw_stored, 16)
            sp.dma_start(wa_sb.rearrange("i (r o) -> i r o", o=D), w_a.rearrange("r i o -> i r o")).then_inc(weights_loaded, 16)
            sp.dma_start(wb_sb.rearrange("i (r o) -> i r o", o=D), rel_w.rearrange("r i o -> i r o")).then_inc(weights_loaded, 16)
            with sp.Fori(0, pl.stages) as t:
                for s in range(2):
                    stage(payd, slot_d, s, t, pl.stages)
            for s in range(2):
                sp.wait_ge(scattered[s], 2 * pl.stages * 16 * CH)
            sp.dma_start(pd[:, 0:NI * 5], bins_dst.rearrange("(p n) f -> p (n f)", p=P)).then_inc(bins_loaded_d, 16)
            for k in range(3):
                sp.wait_ge(table_made, k + 1)
                sp.dma_start(tables[k].rearrange("(b p) f -> p b f", p=P), tab).then_inc(table_stored, 16)

            for k, table in enumerate((table_a, table_b)):
                view = table.rearrange("(b p r) f -> b p (r f)", p=P, b=NB)
                with sp.Fori(0, NB) as b:
                    for c in range(PER[k]):
                        sp.wait_ge(chunk_kept[c], CB[k][c] + b + 1)
                        sp.dma_start(view[b, :, c * 512:(c + 1) * 512], stg[:, c, :]).then_inc(chunk_stored[c], 16)
            sp.wait_ge(out_made, 1)
            sp.dma_start(out[0:FULL * P, :].rearrange("(b p) f -> p b f", p=P), x_sb[:, 0:FULL, :]).then_inc(out_stored, 16)
            if FULL < NB:
                sp.dma_start(out[FULL * P:, :], x_sb[0:pl.last, FULL, :]).then_inc(out_stored, 16)
            sp.wait_ge(out_stored, 16 * (1 + (FULL < NB)))

        @block.gpsimd
        def _(pool):
            pool.sem_inc(gathers_started, CREDIT)
            nc.gpsimd.iota(iota[:, :], pattern=[[1, 512]], base=0, channel_multiplier=0,
                           allow_small_or_imprecise_dtypes=True).then_inc(iota_made, 1)
            nc.gpsimd.iota(lane[:, :], pattern=[[0, 1]], base=0, channel_multiplier=1,
                           allow_small_or_imprecise_dtypes=True).then_inc(iota_made, 1)

            def scatter(bins, slot, words, s, t, uses):
                pool.wait_ge(staged[s], (t + uses + 1) * 16)
                pool.sem_inc(scatters_started, 1)
                for c in range(CH):
                    nc.gpsimd.indirect_dma_start(
                        bins, bass.IndirectOffsetOnAxis(ap=slot[0:LANES, s, c, words:words + 1], axis=0),
                        slot[0:LANES, s, c, 0:words], None).then_inc(scattered[s], 16)

            pool.wait_ge(pads_stored, 32)
            with pool.Fori(0, pl.stages) as t:
                for s in range(2):
                    scatter(bins_src, slot_s, 2, s, t, 0)
            with pool.Fori(0, pl.stages) as t:
                for s in range(2):
                    scatter(bins_dst, slot_d, 5, s, t, pl.stages)

            def gather(ps_):
                used = msg_made if ps_.softmax else summed
                width = ROW if ps_.softmax else D

                def ahead(at):
                    n = ps_.gather + at.g
                    u = at.g + (ps_.gather if ps_.softmax else ps_.every)
                    pool.wait_ge(idx_ready, done(n))
                    pool.wait_ge(used, done(u - RING))
                    pool.sem_inc(gathers_started, 1)
                    for j in range(ITEMS):
                        nc.gpsimd.indirect_dma_start(
                            rows[:, at.slot, j, 0:width], None, ps_.table,
                            bass.IndirectOffsetOnAxis(ap=idx[:, at.slot, j:j + 1], axis=0)).then_inc(gathered[at.slot], 16)
                with pool.Fori(0, NG // 4) as t:
                    for k in range(4):
                        ahead(At(t, k))

            for k, ps_ in enumerate([p_edge] + p_agnn):
                pool.wait_ge(table_stored, 16 * (k + 1))
                gather(ps_)
            for k, ps_ in enumerate(p_plain):
                for c in range(PER[k]):
                    pool.wait_ge(chunk_stored[c], 16 * (CB[k][c] + NB))
                gather(ps_)

        @block.scalar
        def _(act):
            for s in (idx_ready, hot_t_made, pen_made, scored_b, keep_made, exp_made, ht_kept):
                act.sem_inc(s, CREDIT)
            for k in range(8):
                act.wait_ge(relw_made, k + 1)
                nc.scalar.copy(relw_sb[:, k * 512:(k + 1) * 512], pbig[0:pl.rel_b, k % 4, :]).then_inc(relw_kept, 1)
            asked = [0]

            def root(col):
                asked[0] += 1
                act.wait_ge(dve_asks_act, asked[0])
                nc.scalar.activation(col, col, ACT.Sqrt).then_inc(act_answers, 1)

            def work(ps_):
                e = ps_.every

                def ahead(at):
                    if ps_.kind != SOURCE:
                        act.wait_ge(gathered[at.slot], (at.rnd + ps_.rounds) * 64)
                        nc.scalar.copy(idx[:, at.slot, :], pdi[:, bass.ds(at.g * 4, 4), ps_.column]).then_inc(idx_ready, 1)
                    if not ps_.softmax:
                        return
                    act.wait_ge(turned, done(e + at.g))
                    act.wait_ge(edge_max, done(e + at.g - RING))
                    nc.scalar.copy(hot_t[:, at.slot, :, :].rearrange("p j e -> p (j e)"), p_t[:, at.half, :]).then_inc(hot_t_made, 1)
                    act.wait_ge(spread, done(e + at.g - 2))
                    nc.scalar.activation(pen_t[:, at.half, :], p_t[:, at.half, :], ACT.Identity,
                                         bias=neg_big[:, 0:1], scale=BIG).then_inc(pen_made, 1)

                def middle(at):
                    if not ps_.softmax:
                        return
                    act.wait_ge(spread, done(e + at.g - 2))
                    if ps_.kind == AGNN:
                        act.wait_ge(scored, done(ps_.own + at.g))
                        nc.scalar.copy(score_b[:, at.half, :], score[:, at.half, :]).then_inc(scored_b, 1)
                    else:
                        nc.scalar.copy(score_b[:, at.half, :], ps_.weight[:, bass.ds(at.g * 4, 4)]).then_inc(scored_b, 1)

                def late(at):
                    if not ps_.softmax:
                        return
                    act.wait_ge(dropped, done(e + at.g))
                    act.wait_ge(added, done(e + at.g - 2))
                    last = nc.scalar.activation(keep[:, at.half, 0:1], drop[:, at.half:at.half + 1], ACT.Exp)
                    if ps_.kind == EDGE:
                        last = nc.scalar.activation(keep[:, at.half, 1:2], drop[:, at.half:at.half + 1], ACT.Exp, scale=0.5)
                    last.then_inc(keep_made, 1)

                def behind(at):
                    if not ps_.softmax:
                        return
                    act.wait_ge(shift_made, done(e + at.g))
                    if ps_.kind == SOURCE:
                        act.wait_ge(summed, done(e + at.g - 2))
                    else:
                        act.wait_ge(msg_made, done(ps_.gather + at.g - 2))
                    if ps_.kind == EDGE:
                        nc.scalar.activation(expd[:, at.half, :, :], shifted[:, at.half, :, :], ACT.Exp).then_inc(exp_made, 1)
                    else:
                        nc.scalar.activation(expd[:, at.half, 0, :], shifted[:, at.half, 0, :], ACT.Exp).then_inc(exp_made, 1)

                run_pass(act, ahead, middle, behind, late)

            act.wait_ge(consts_made, 1)
            root(col_a[:, :])
            act.wait_ge(bins_loaded_s, 16)
            work(p_source)
            asked[0] += 1
            act.wait_ge(dve_asks_act, asked[0])
            nc.scalar.activation(col_b[:, :], col_b[:, :], ACT.Ln).then_inc(act_answers, 1)
            act.wait_ge(bins_loaded_d, 16)
            work(p_edge)
            root(col_a[:, :])
            root(col_a[:, :])
            root(col_a[:, :])
            work(p_agnn[0])
            root(col_a[:, :])
            work(p_agnn[1])

            def build(k):
                def one(b, half):
                    n = k * NB + b
                    act.wait_ge(blk_turned, done(n))
                    act.wait_ge(chunk_made[PER[k] - 1], done(CB[k][-1] + b - 2))
                    nc.scalar.copy(ht[:, half, :], p_turn[0:D, half, :]).then_inc(ht_kept, 1)
                    for c in range(1, PER[k], 2):
                        act.wait_ge(chunk_made[c], done(CB[k][c] + b))
                        act.wait_ge(chunk_stored[c], (CB[k][c] + b) * 16)
                        nc.scalar.copy(stg[:, c, :], pbig[:, c, :]).then_inc(chunk_kept[c], 1)
                over_blocks(act, one)

            root(col_a[:, :])
            build(0)
            work(p_plain[0])
            root(col_a[:, :])
            build(1)
            work(p_plain[1])

        @block.vector
        def _(dve):
            for s in (hot_made, multiplied, dotted, scored, group_max, max_made, dropped, max_kept,
                      shift_made, unsourced, msg_made, added, blk_copied, self_added):
                dve.sem_inc(s, CREDIT)
            steps = [0]

            def link(ins):
                steps[0] += 1
                ins.then_inc(dve_step, 1)
                dve.wait_ge(dve_step, steps[0])

            def linked(t, per, k):
                return steps[0] + t * per + k

            asked = [0]

            def ask(ins):
                asked[0] += 1
                ins.then_inc(dve_asks_act, 1)
                dve.wait_ge(act_answers, asked[0])

            v = nc.vector
            dve.wait_ge(iota_made, 2)
            v.tensor_scalar(ident[:, :], iota[:, 0:P], lane[:, 0:1], None, ALU.is_equal)
            v.tensor_scalar(ident_b[:, :], iota[:, 0:P], lane[:, 0:1], None, ALU.is_equal)
            v.tensor_scalar(before[:, :], iota[:, 0:P], lane[:, 0:1], None, ALU.is_gt)
            v.memset(ones[:, :], 1.0)
            v.memset(h_blk[:, :, :], 0.0)
            v.memset(bin_zero[:, :], 0.0)
            v.memset(run_max[:, :], -BIG)
            v.memset(out_sum[:, :], 0.0)
            link(v.memset(neg_big[:, :], -BIG))
            v.memset(lane_bin[:, :], 0.0).then_inc(consts_made, 1)
            v.memset(psf[:, :, 0], -1.0)
            v.memset(psf[:, :, 1], 0.0).then_inc(pads_made, 1)
            dve.wait_ge(relw_stored, 16)
            v.memset(pdi[:, :, 0], pl.nodes)
            v.memset(pdf[:, :, 1], -1.0)
            v.memset(pdf[:, :, 2], 0.0)
            v.memset(pdi[:, :, 3], pl.nodes * pl.rel_a)
            v.memset(pdi[:, :, 4], pl.nodes * pl.rel_b).then_inc(pads_made, 1)

            def sort(k, key, local, addr, blocks):
                link(v.tensor_scalar(hot_i, key, 7, None, ALU.arith_shift_right))
                link(v.tensor_copy(bin_c, hot_i))
                link(v.tensor_scalar(hot_i, key, 127, None, ALU.bitwise_and))
                link(v.tensor_copy(local, hot_i))
                with dve.Fori(0, NB) as b:
                    v.tensor_scalar(hot_c, bin_c, iota[0:LANES, bass.ds(b, 1)], None, ALU.is_equal, ALU.add,
                                    accum_out=lane_bin[0:LANES, bass.ds(b, 1)]).then_inc(dve_step, 1)
                    dve.wait_ge(dve_step, linked(b, 1, 1))
                steps[0] += NB
                v.engine_nop().then_inc(counted, 1)
                dve.wait_ge(offsets_made, k + 1)
                link(v.tensor_scalar(bin_groups_i[:, :], p_cnt[:, 64:64 + NB], float(ITEMS * P - 1), None, ALU.add))
                link(v.tensor_scalar(bin_groups_i[:, :], bin_groups_i[:, :], 9, None, ALU.arith_shift_right))
                link(v.tensor_copy(bin_groups[:, :], bin_groups_i[:, :]))
                link(v.tensor_tensor_scan(bin_first[:, :], bin_groups[:, :], bin_zero[:, :], 0.0, ALU.add, ALU.add))
                link(v.tensor_tensor(bin_first[:, :], bin_first[:, :], bin_groups[:, :], ALU.subtract))
                v.engine_nop().then_inc(first_made, 1)
                link(v.tensor_scalar(bin_from[:, :], bin_first[:, :], float(ITEMS * P), -1.0, ALU.mult, ALU.add))
                link(v.tensor_tensor(bin_from[0:LANES, :], bin_from[0:LANES, :], p_cnt[0:LANES, 0:NB], ALU.add))
                dve.wait_ge(first_col_made, k + 1)
                link(v.tensor_copy(first_col[:, :], p_col[0:NB, 0:1]))
                v.tensor_scalar(reached[:, :], iota[0:NB, 0:NG], first_col[:, 0:1], None, ALU.is_ge).then_inc(reached_made, 1)
                dve.wait_ge(block_made, k + 1)
                v.tensor_scalar(blocks[:, :], pbig[0:1, 0, 0:NG], -1.0, None, ALU.add).then_inc(blocks_ready, 1)
                link(v.memset(pos_c, 0.0))
                with dve.Fori(0, NB) as b:
                    v.tensor_scalar(hot_c, bin_c, iota[0:LANES, bass.ds(b, 1)], None, ALU.is_equal).then_inc(dve_step, 1)
                    dve.wait_ge(dve_step, linked(b, 4, 1))
                    v.tensor_tensor_scan(run_c, hot_c, hot_c, bin_from[0:LANES, bass.ds(b, 1)], ALU.add, ALU.bypass).then_inc(dve_step, 1)
                    dve.wait_ge(dve_step, linked(b, 4, 2))
                    v.tensor_tensor(hot_c, hot_c, run_c, ALU.mult).then_inc(dve_step, 1)
                    dve.wait_ge(dve_step, linked(b, 4, 3))
                    v.tensor_tensor(pos_c, pos_c, hot_c, ALU.add).then_inc(dve_step, 1)
                    dve.wait_ge(dve_step, linked(b, 4, 4))
                steps[0] += 4 * NB
                link(v.tensor_copy(hot_i, pos_c))
                link(v.tensor_scalar(run_i, hot_i, 127, None, ALU.bitwise_and))
                link(v.tensor_scalar(hot_i, hot_i, 7, None, ALU.arith_shift_right))
                link(v.scalar_tensor_tensor(out=addr, in0=run_i, scalar=float(NI), in1=hot_i, op0=ALU.mult, op1=ALU.add))

            dve.wait_ge(loaded_ids, 32)
            dve.wait_ge(loaded_w, 16)
            v.tensor_copy(paysf[:, :, 1], wgt_c)
            sort(0, src_c, paysf[:, :, 0], pays[:, :, 2], block_s)
            v.engine_nop().then_inc(pay_ready, 1)
            dve.wait_ge(loaded_types, 16)
            v.tensor_copy(payd[:, :, 0], src_c)
            v.tensor_copy(paydf[:, :, 2], wgt_c)
            v.scalar_tensor_tensor(out=payd[:, :, 3], in0=src_c, scalar=float(pl.rel_a), in1=typ_c,
                                   op0=ALU.mult, op1=ALU.add).then_inc(types_used, 1)
            sort(1, dst_c, paydf[:, :, 1], payd[:, :, 5], block_d)
            dve.wait_ge(loaded_types, 32)
            link(v.scalar_tensor_tensor(out=payd[:, :, 4], in0=src_c, scalar=float(pl.rel_b), in1=typ_c,
                                        op0=ALU.mult, op1=ALU.add))
            v.memset(x_sb[:, :, :], 0.0).then_inc(x_cleared, 1)
            v.engine_nop().then_inc(pay_ready, 1)

            def bc(col, n=D):
                return col.unsqueeze(2).to_broadcast([P, NB, n])

            def layer_norm():
                link(v.reduce_sum(col_a[:, :], x_sb[:, :, :], AX))
                link(v.tensor_scalar(col_a[:, :], col_a[:, :], 1.0 / D, None, ALU.mult))
                link(v.tensor_tensor(h_sb[:, :, :], x_sb[:, :, :], bc(col_a[:, :]), ALU.subtract))
                link(v.tensor_tensor(sq[:, :, :], h_sb[:, :, :], h_sb[:, :, :], ALU.mult))
                link(v.reduce_sum(col_a[:, :], sq[:, :, :], AX))
                ask(v.tensor_scalar(col_a[:, :], col_a[:, :], 1.0 / D, LN_EPS, ALU.mult, ALU.add))
                link(v.reciprocal(col_a[:, :], col_a[:, :]))
                link(v.tensor_tensor(h_sb[:, :, :], h_sb[:, :, :], bc(col_a[:, :]), ALU.mult))
                link(v.tensor_scalar(h_sb[:, :, :], h_sb[:, :, :], 0.0, None, ALU.max))

            def agnn_table(k):
                link(v.tensor_tensor(sq[:, :, :], h_sb[:, :, :], h_sb[:, :, :], ALU.mult))
                ask(v.reduce_sum(col_a[:, :], sq[:, :, :], AX))
                link(v.tensor_scalar(col_a[:, :], col_a[:, :], NORM_EPS, None, ALU.max))
                link(v.reciprocal(col_a[:, :], col_a[:, :]))
                link(v.tensor_tensor(sq[:, :, :], h_sb[:, :, :], bc(col_a[:, :]), ALU.mult))
                for part in range(3):
                    link(v.tensor_copy(unit3[:, part, :, :], sq[:, :, :]))
                    if part < 2:
                        link(v.tensor_tensor(sq[:, :, :], sq[:, :, :], unit3[:, part, :, :], ALU.subtract))
                v.engine_nop().then_inc(units_made, 1)
                v.tensor_scalar(tab[:, :, D], col_a[:, :], beta_sb[:, k:k + 1], None, ALU.mult)
                v.tensor_copy(tab[:, :, 0:D], h_sb[:, :, :]).then_inc(table_made, 1)

            def clear_sums():
                v.memset(run_max[:, :], -BIG)
                link(v.memset(acc[:, :, :], 0.0))

            def work(ps_):
                e = ps_.every

                def block_of(at):
                    return dve.value_load(ps_.block[0:1, bass.ds(at.g, 1)], min_val=0, max_val=NB - 1)

                def ahead(at):
                    dve.wait_ge(summed, done(e + at.g - RING))
                    v.tensor_tensor(hot[:, at.slot, :, :], iota[:, 0:P].unsqueeze(1).to_broadcast([P, ITEMS, P]),
                                    ps_.local[:, bass.ds(at.g * 4, 4)].unsqueeze(2).to_broadcast([P, ITEMS, P]),
                                    ALU.is_equal).then_inc(hot_made, 1)

                def middle(at):
                    if ps_.kind != AGNN:
                        return
                    a = ps_.own + at.g
                    here = rows[:, at.slot, :, :]
                    dve.wait_ge(gathered[at.slot], (at.rnd + ps_.rounds + 1) * 64)
                    dve.wait_ge(dst_rows, done(a))
                    dve.wait_ge(dotted, done(a - 1))
                    v.tensor_tensor(prod[:, at.half, :, :], here[:, :, 0:D], p_row[:, at.half, :, :], ALU.mult).then_inc(multiplied, 1)
                    dve.wait_ge(multiplied, done(a))
                    v.reduce_sum(dot[:, at.half, :], prod[:, at.half, :, :], AX).then_inc(dotted, 1)
                    dve.wait_ge(dotted, done(a))
                    dve.wait_ge(scored_b, done(e + at.g - 2))
                    v.tensor_tensor(score[:, at.half, :], dot[:, at.half, :], here[:, :, D], ALU.mult).then_inc(scored, 1)

                def late(at):
                    if not ps_.softmax:
                        return
                    b = block_of(at)
                    dve.wait_ge(spread, done(e + at.g))
                    v.reduce_max(gmax[:, at.half:at.half + 1], p_v[:, at.half, :], AX).then_inc(group_max, 1)
                    dve.wait_ge(group_max, done(e + at.g))
                    dve.wait_ge(max_kept, done(e + at.g - 1))
                    dve.wait_ge(edge_max, done(e + at.g - 2))
                    v.tensor_tensor(new_max[:, at.half:at.half + 1], run_max[:, bass.ds(b, 1)], gmax[:, at.half:at.half + 1],
                                    ALU.max).then_inc(max_made, 1)
                    dve.wait_ge(max_made, done(e + at.g))
                    dve.wait_ge(keep_made, done(e + at.g - 2))
                    v.tensor_tensor(drop[:, at.half:at.half + 1], run_max[:, bass.ds(b, 1)], new_max[:, at.half:at.half + 1],
                                    ALU.subtract).then_inc(dropped, 1)
                    dve.wait_ge(dropped, done(e + at.g))
                    v.tensor_scalar(run_max[:, bass.ds(b, 1)], new_max[:, at.half:at.half + 1], 1.0, None, ALU.mult).then_inc(max_kept, 1)

                def behind(at):
                    here = rows[:, at.slot, :, :]
                    half = at.half
                    w = ps_.weight[:, bass.ds(at.g * 4, 4)]
                    if ps_.softmax:
                        dve.wait_ge(exp_made, done(e + at.g - 2))
                        if ps_.kind == EDGE:
                            dve.wait_ge(gathered[at.slot], (at.rnd + ps_.rounds + 1) * 64)
                            v.tensor_tensor(less_src[:, half, :], w, here[:, :, D], ALU.subtract).then_inc(unsourced, 1)
                        dve.wait_ge(edge_max, done(e + at.g))
                        if ps_.kind == AGNN:
                            dve.wait_ge(scored, done(ps_.own + at.g))
                            v.tensor_tensor(shifted[:, half, 0, :], score[:, half, :], p_max[:, 0:ITEMS], ALU.subtract).then_inc(shift_made, 1)
                        elif ps_.kind == SOURCE:
                            v.tensor_tensor(shifted[:, half, 0, :], w, p_max[:, 0:ITEMS], ALU.subtract).then_inc(shift_made, 1)
                        else:
                            v.tensor_tensor(shifted[:, half, 0, :], w, p_max[:, 0:ITEMS], ALU.subtract)
                            dve.wait_ge(unsourced, done(at.g))
                            v.scalar_tensor_tensor(out=shifted[:, half, 1, :], in0=p_max[:, 0:ITEMS], scalar=-0.5,
                                                   in1=less_src[:, half, :], op0=ALU.mult, op1=ALU.add).then_inc(shift_made, 1)
                    if ps_.kind in (EDGE, AGNN):
                        m = ps_.gather + at.g
                        dve.wait_ge(exp_made, done(e + at.g))
                        dve.wait_ge(summed, done(e + at.g - 2))
                        v.tensor_copy(msg[:, half, :, D], expd[:, half, 0, :])
                        v.tensor_tensor(msg[:, half, :, 0:D], here[:, :, 0:D],
                                        expd[:, half, int(ps_.kind == EDGE), :].unsqueeze(2).to_broadcast([P, ITEMS, D]),
                                        ALU.mult).then_inc(msg_made, 1)
                    b = block_of(at)
                    dve.wait_ge(summed, done(e + at.g))
                    dve.wait_ge(added, done(e + at.g - 1))
                    if ps_.softmax:
                        dve.wait_ge(keep_made, done(e + at.g))
                    if ps_.kind == SOURCE:
                        v.scalar_tensor_tensor(out=out_sum[:, bass.ds(b, 1)], in0=out_sum[:, bass.ds(b, 1)], scalar=keep[:, half, 0:1],
                                               in1=p_sum[:, 0:1], op0=ALU.mult, op1=ALU.add).then_inc(added, 1)
                    elif ps_.kind == EDGE:
                        v.scalar_tensor_tensor(out=acc[:, b, 0:D], in0=acc[:, b, 0:D], scalar=keep[:, half, 1:2],
                                               in1=p_sum[:, 0:D], op0=ALU.mult, op1=ALU.add)
                        v.scalar_tensor_tensor(out=acc[:, b, D:ROW], in0=acc[:, b, D:ROW], scalar=keep[:, half, 0:1],
                                               in1=p_sum[:, D:ROW], op0=ALU.mult, op1=ALU.add).then_inc(added, 1)
                    elif ps_.kind == AGNN:
                        v.scalar_tensor_tensor(out=acc[:, b, :], in0=acc[:, b, :], scalar=keep[:, half, 0:1],
                                               in1=p_sum[:, 0:ROW], op0=ALU.mult, op1=ALU.add).then_inc(added, 1)
                    else:
                        v.tensor_tensor(acc[:, b, :], acc[:, b, :], p_sum[:, 0:ROW], ALU.add).then_inc(added, 1)

                run_pass(dve, ahead, middle, behind, late)
                dve.wait_ge(added, done(e + NG - 1))

            def build(k):
                def one(b, half):
                    n = k * NB + b
                    dve.wait_ge(blk_turned, done(n - 2))
                    v.tensor_scalar(h_blk[:, half, 0:D], h_sb[:, b, :], 1.0, None, ALU.mult).then_inc(blk_copied, 1)
                    for c in range(0, PER[k], 2):
                        dve.wait_ge(chunk_made[c], done(CB[k][c] + b))
                        dve.wait_ge(chunk_stored[c], (CB[k][c] + b) * 16)
                        v.tensor_copy(stg[:, c, :], pbig[:, c, :]).then_inc(chunk_kept[c], 1)
                    if k == 1:
                        dve.wait_ge(self_made, done(b))
                        v.tensor_tensor(x_sb[:, b, :], x_sb[:, b, :], p_sum[:, 0:D], ALU.add).then_inc(self_added, 1)
                over_blocks(dve, one)

            for _ in range(1):
                dve.wait_ge(x_loaded, 16 * (1 + (FULL < NB)))
                layer_norm()
            dve.wait_ge(bins_loaded_s, 16)
            work(p_source)
            link(v.tensor_scalar(col_b[:, :], out_sum[:, :], 2.0 ** -60, None, ALU.max))
            link(v.tensor_scalar(col_c[:, :], out_sum[:, :], 2.0 ** -59, 0.5, ALU.is_gt, ALU.mult))
            ask(v.engine_nop())
            link(v.tensor_tensor(col_b[:, :], col_b[:, :], run_max[:, :], ALU.add))
            link(v.tensor_tensor(tab[:, :, D], col_b[:, :], col_c[:, :], ALU.mult))
            v.tensor_copy(tab[:, :, 0:D], h_sb[:, :, :]).then_inc(table_made, 1)
            dve.wait_ge(bins_loaded_d, 16)
            clear_sums()
            work(p_edge)
            link(v.tensor_scalar(col_a[:, :], acc[:, :, D], 1e-30, None, ALU.max))
            ask(v.engine_nop())
            link(v.reciprocal(col_a[:, :], col_a[:, :]))
            link(v.tensor_tensor(acc[:, :, 0:D], acc[:, :, 0:D], bc(col_a[:, :]), ALU.mult))
            link(v.tensor_tensor(x_sb[:, :, :], x_sb[:, :, :], acc[:, :, 0:D], ALU.add))

            layer_norm()
            dve.wait_ge(loaded_small, 48)
            for k in range(2):
                agnn_table(k)
                clear_sums()
                work(p_agnn[k])
                link(v.tensor_scalar(col_a[:, :], acc[:, :, D], 1e-30, None, ALU.max))
                link(v.reciprocal(col_a[:, :], col_a[:, :]))
                link(v.tensor_tensor(h_sb[:, :, :], acc[:, :, 0:D], bc(col_a[:, :]), ALU.mult))
                link(v.tensor_scalar(h_sb[:, :, :], h_sb[:, :, :], 0.0, None, ALU.max))
            link(v.tensor_tensor(x_sb[:, :, :], x_sb[:, :, :], h_sb[:, :, :], ALU.add))

            layer_norm()
            dve.wait_ge(weights_loaded, 32)
            build(0)
            v.memset(rows[:, :, :, D], 1.0)
            clear_sums()
            work(p_plain[0])
            link(v.tensor_tensor(x_sb[:, :, :], x_sb[:, :, :], acc[:, :, 0:D], ALU.add))

            layer_norm()
            link(v.tensor_tensor(x_sb[:, :, :], x_sb[:, :, :], bias_sb[:, :].unsqueeze(1).to_broadcast([P, NB, D]), ALU.add))
            build(1)
            clear_sums()
            work(p_plain[1])
            link(v.tensor_scalar(col_a[:, :], acc[:, :, D], 1.0, None, ALU.max))
            link(v.reciprocal(col_a[:, :], col_a[:, :]))
            link(v.tensor_tensor(acc[:, :, 0:D], acc[:, :, 0:D], bc(col_a[:, :]), ALU.mult))
            v.tensor_tensor(x_sb[:, :, :], x_sb[:, :, :], acc[:, :, 0:D], ALU.add).then_inc(out_made, 1)

        @block.tensor
        def _(pe):
            for s in (turned, dst_rows, spread, edge_max, summed, blk_turned, self_made, *chunk_made):
                pe.sem_inc(s, CREDIT)
            mm = nc.tensor.matmul
            pe.wait_ge(loaded_basis, 32)
            for k in range(8):
                if k >= 4:
                    pe.wait_ge(relw_kept, k - 3)
                mm(pbig[0:pl.rel_b, k % 4, :], coeff_t[:, :], basis_sb[:, k * 512:(k + 1) * 512],
                   start=True, stop=True).then_inc(relw_made, 1)
            pe.wait_ge(consts_made, 1)
            pe.wait_ge(relw_kept, 8)
            for k in range(2):
                pe.wait_ge(counted, k + 1)
                mm(p_cnt[0:LANES, 0:NB], before[0:LANES, 0:LANES], lane_bin[0:LANES, :], start=True, stop=True)
                mm(p_cnt[:, 64:64 + NB], ones[0:LANES, :], lane_bin[0:LANES, :], start=True, stop=True).then_inc(offsets_made, 1)
                pe.wait_ge(first_made, k + 1)
                mm(p_col[0:NB, 0:1], bin_first[0:1, :], ones[0:1, 0:1], start=True, stop=True).then_inc(first_col_made, 1)
                pe.wait_ge(reached_made, k + 1)
                mm(pbig[0:1, 0, 0:NG], ones[0:NB, 0:1], reached[:, :], start=True, stop=True).then_inc(block_made, 1)

            def work(ps_):
                e = ps_.every

                def ahead(at):
                    if not ps_.softmax:
                        return
                    pe.wait_ge(hot_made, done(e + at.g))
                    pe.wait_ge(pen_made, done(e + at.g - 2))
                    for j in range(ITEMS):
                        last = nc.tensor.transpose(p_t[:, at.half, j * P:(j + 1) * P], hot[:, at.slot, j, :], ident[:, :])
                    last.then_inc(turned, 1)

                def middle(at):
                    if ps_.kind != AGNN:
                        return
                    b = pe.value_load(ps_.block[0:1, bass.ds(at.g, 1)], min_val=0, max_val=NB - 1)
                    pe.wait_ge(hot_t_made, done(e + at.g))
                    pe.wait_ge(multiplied, done(ps_.own + at.g - 2))
                    for j in range(ITEMS):
                        for part in range(3):
                            last = mm(p_row[:, at.half, j, :], hot_t[:, at.slot, j, :], unit3[:, part, b, :],
                                      start=part == 0, stop=part == 2)
                    last.then_inc(dst_rows, 1)

                def late(at):
                    if not ps_.softmax:
                        return
                    pe.wait_ge(pen_made, done(e + at.g))
                    pe.wait_ge(group_max, done(e + at.g - 2))
                    mm(p_v[:, at.half, :], ident_b[:, :], pen_t[:, at.half, :], start=True, stop=False)
                    pe.wait_ge(scored_b, done(e + at.g))
                    for j in range(ITEMS):
                        last = mm(p_v[:, at.half, j * P:(j + 1) * P], score_b[:, at.half, j:j + 1].to_broadcast([P, P]),
                                  ident_b[:, :], start=False, stop=j == ITEMS - 1)
                    last.then_inc(spread, 1)

                def behind(at):
                    if ps_.softmax:
                        pe.wait_ge(max_made, done(e + at.g))
                        pe.wait_ge(hot_t_made, done(e + at.g))
                        pe.wait_ge(shift_made, done(e + at.g - 1))
                        for j in range(ITEMS):
                            last = mm(p_max[:, j:j + 1], hot_t[:, at.slot, j, :], new_max[:, at.half:at.half + 1],
                                      start=True, stop=True)
                        last.then_inc(edge_max, 1)
                    pe.wait_ge(added, done(e + at.g - 1))
                    pe.wait_ge(hot_made, done(e + at.g))
                    if ps_.kind == SOURCE:
                        pe.wait_ge(exp_made, done(e + at.g))
                    elif ps_.softmax:
                        pe.wait_ge(msg_made, done(ps_.gather + at.g))
                    else:
                        pe.wait_ge(gathered[at.slot], (at.rnd + ps_.rounds + 1) * 64)
                    for j in range(ITEMS):
                        if ps_.kind == SOURCE:
                            given = expd[:, at.half, 0, j:j + 1]
                        elif ps_.softmax:
                            given = msg[:, at.half, j, :]
                        else:
                            given = rows[:, at.slot, j, :]
                        last = mm(p_sum[:, 0:given.shape[1]], hot[:, at.slot, j, :], given,
                                  start=j == 0, stop=j == ITEMS - 1)
                    last.then_inc(summed, 1)

                run_pass(pe, ahead, middle, behind, late)

            def build(k):
                weights = (wa_sb, wb_sb)[k]

                def one(b, half):
                    n = k * NB + b
                    pe.wait_ge(blk_copied, done(n))
                    pe.wait_ge(ht_kept, done(n - 2))
                    nc.tensor.transpose(p_turn[:, half, :], h_blk[:, half, :], ident[:, :]).then_inc(blk_turned, 1)
                    pe.wait_ge(ht_kept, done(n))
                    if k == 1:
                        pe.wait_ge(self_added, done(b - 1))
                        mm(p_sum[:, 0:D], ht[:, half, :], wself_sb[:, :], start=True, stop=True).then_inc(self_made, 1)
                    for c in range(PER[k]):
                        pe.wait_ge(chunk_kept[c], CB[k][c] + b)
                        mm(pbig[:, c, :], ht[:, half, :], weights[:, c * 512:(c + 1) * 512],
                           start=True, stop=True).then_inc(chunk_made[c], 1)
                over_blocks(pe, one)

            pe.wait_ge(blocks_ready, 1)
            work(p_source)
            pe.wait_ge(blocks_ready, 2)
            work(p_edge)
            for k in range(2):
                pe.wait_ge(units_made, k + 1)
                work(p_agnn[k])
            pe.wait_ge(weights_loaded, 32)
            build(0)
            work(p_plain[0])
            build(1)
            work(p_plain[1])


def kernel(x, src, dst, edge_type_16, edge_type_32, edge_weight, L1_gnn_beta, L2_gnn_weight,
           L3_gnn_basis, L3_gnn_coeff, L3_gnn_self_weight, L3_gnn_bias):
    import numpy as np
    import concourse.bacc as bacc
    from concourse.bass_utils import run_bass_kernel_spmd

    given = dict(x=x, src=src, dst=dst, type_a=edge_type_16, type_b=edge_type_32, weight=edge_weight,
                 beta=L1_gnn_beta, w_a=L2_gnn_weight, basis=L3_gnn_basis, coeff=L3_gnn_coeff,
                 w_self=L3_gnn_self_weight, bias=L3_gnn_bias)
    nc = bacc.Bacc("TRN2", target_bir_lowering=False, num_devices=1)
    arrays, args = {}, []
    for name, a in given.items():
        a = np.ascontiguousarray(a)
        arrays[f"in_{name}"] = a
        args.append(nc.dram_tensor(f"in_{name}", a.shape, mybir.dt.from_np(a.dtype), kind="ExternalInput").ap())
    out = nc.dram_tensor("out", np.shape(x), F32, kind="ExternalOutput").ap()
    gnn_program(nc, *args, out)
    r = run_bass_kernel_spmd(nc, [arrays], core_ids=[0])
    return r.results[0]["out"]
```

```python
import concourse.bass as bass
from concourse import mybir
from contextlib import ExitStack

F32 = mybir.dt.float32
BF16 = mybir.dt.bfloat16
I32 = mybir.dt.int32
ALU = mybir.AluOpType
ACT = mybir.ActivationFunctionType
AX = mybir.AxisListType.X

P = 128
ITEMS = 4
RING = 6
CREDIT = 8
D = 64
ROW = D + 1
BIG = float(2 ** 100)
LN_EPS = 1e-5
NORM_EPS = 1e-12


class Plan:

    def __init__(self, nodes, edges, rel_a, rel_b, bases):
        self.nodes, self.edges = nodes, edges
        self.rel_a, self.rel_b, self.bases = rel_a, rel_b, bases
        self.blocks = -(-nodes // P)
        self.last = nodes - (self.blocks - 1) * P
        self.lanes = max(d for d in range(1, P + 1) if edges % d == 0)
        self.cols = edges // self.lanes
        self.stage = max(c for c in range(1, 21) if self.cols % (2 * c) == 0)
        self.stages = self.cols // (2 * self.stage)
        most = (edges + self.blocks * (ITEMS * P - 1)) // (ITEMS * P)
        self.groups = most
        self.items = self.groups * ITEMS


class At:

    def __init__(self, rnd, slot):
        self.rnd, self.slot = rnd, slot
        self.two, self.three = slot % 2, slot % 3
        self.g = rnd * RING + slot


def gnn_program(nc, x, src, dst, type_a, type_b, weight, beta, w_a, basis, coeff, w_self, bias, out):
    pl = Plan(x.shape[0], src.shape[0], w_a.shape[0], coeff.shape[0], basis.shape[0])
    NB, LANES, COLS, NI, NG = pl.blocks, pl.lanes, pl.cols, pl.items, pl.groups
    CH = pl.stage
    FULL = NB - 1 if pl.last < P else NB

    def scratch(name, shape, dt=F32):
        return nc.dram_tensor(name, shape, dt).ap()

    bins_dst = scratch("bins_dst", (P * NI, 5), I32)
    bins_src = scratch("bins_src", (P * NI, 2), I32)
    tables = [scratch(f"table{k}", (NB * P, ROW)) for k in range(3)]
    table_a = scratch("table_a", (NB * P * pl.rel_a, D))
    table_b = scratch("table_b", (NB * P * pl.rel_b, D))
    rel_w = scratch("rel_w", (pl.rel_b, D, D))

    ctx = ExitStack()
    with ctx:
        def sb(name, shape, dt=F32):
            return ctx.enter_context(nc.sbuf_tensor(name, shape, dt))

        def sem(name):
            return ctx.enter_context(nc.semaphore(name))

        ZW = max(8 * COLS, 2 * NB * D + NB * ROW + (RING + 2) * ITEMS * ROW + RING * ITEMS * P // 2)
        Z = sb("Z", [P, ZW])
        pay_d = sb("pay_d", [P, max(COLS * 6, NB * ROW + 3 * NB * D // 2 + D)], I32)
        pay_s = sb("pay_s", [P, max(COLS * 3, (pl.rel_a + pl.rel_b) * D)], I32)
        pd = sb("pd", [P, max(NI * 5, 2 * D * D)], I32)
        ps = sb("ps", [P, max(NI * 2, 4 * 512)], I32)

        def zcol(k, dt=F32):
            return Z[0:LANES, k * COLS:(k + 1) * COLS].bitcast(dt) if dt != F32 else Z[0:LANES, k * COLS:(k + 1) * COLS]

        src_c, dst_c, typ_c = zcol(0, I32), zcol(1, I32), zcol(2, I32)
        wgt_c, bin_c, pos_c, hot_c, run_c = zcol(3), zcol(4), zcol(5), zcol(6), zcol(7)
        hot_i, run_i, pos_i = zcol(6, I32), zcol(7, I32), zcol(5, I32)
        payd = pay_d[0:LANES, 0:COLS * 6].rearrange("p (c f) -> p c f", f=6)
        paydf = pay_d[0:LANES, 0:COLS * 6].bitcast(F32).rearrange("p (c f) -> p c f", f=6)
        pays = pay_s[0:LANES, 0:COLS * 3].rearrange("p (c f) -> p c f", f=3)
        paysf = pay_s[0:LANES, 0:COLS * 3].bitcast(F32).rearrange("p (c f) -> p c f", f=3)
        slot_d = sb("slot_d", [P, 2, CH, 6], I32)
        slot_s = sb("slot_s", [P, 2, CH, 3], I32)
        pdi = pd[:, 0:NI * 5].rearrange("p (n f) -> p n f", f=5)
        pdf = pd[:, 0:NI * 5].bitcast(F32).rearrange("p (n f) -> p n f", f=5)
        psf = ps[:, 0:NI * 2].bitcast(F32).rearrange("p (n f) -> p n f", f=2)
        basis_sb = pd[0:pl.bases, 0:D * D].bitcast(F32)
        relw_sb = pd[0:pl.rel_b, D * D:2 * D * D].bitcast(F32)
        o = 0
        x_sb = Z[:, o:o + NB * D].rearrange("p (b f) -> p b f", f=D)
        o += NB * D
        h_sb = Z[:, o:o + NB * D].rearrange("p (b f) -> p b f", f=D)
        o += NB * D
        tab_flat = Z[:, o:o + NB * ROW]
        tab = tab_flat.rearrange("p (b f) -> p b f", f=ROW)
        sq = Z[:, o:o + NB * D].rearrange("p (b f) -> p b f", f=D)
        o += NB * ROW
        rows = Z[:, o:o + RING * ITEMS * ROW].rearrange("p (s j f) -> p s j f", s=RING, j=ITEMS)
        o += RING * ITEMS * ROW
        msg = Z[:, o:o + 2 * ITEMS * ROW].rearrange("p (s j f) -> p s j f", s=2, j=ITEMS)
        o += 2 * ITEMS * ROW
        hot = Z[:, o:o + RING * ITEMS * P // 2].bitcast(BF16).rearrange("p (s j n) -> p s j n", s=RING, j=ITEMS)
        acc = pay_d[:, 0:NB * ROW].bitcast(F32).rearrange("p (b f) -> p b f", f=ROW)
        unit3 = pay_d[:, NB * ROW:NB * ROW + 3 * NB * D // 2].bitcast(BF16).rearrange("p (k b f) -> p k b f", k=3, f=D)
        wa_sb = pay_s[0:D, 0:pl.rel_a * D].bitcast(F32)
        wb_sb = pay_s[0:D, pl.rel_a * D:(pl.rel_a + pl.rel_b) * D].bitcast(F32)
        stg = ps[:, 0:4 * 512].bitcast(F32).rearrange("p (s c) -> p s c", s=4)

        iota = sb("iota", [P, 512])
        iota_b = sb("iota_b", [P, P], BF16)
        lane = sb("lane", [P, 1])
        ident = sb("ident", [P, P])
        ident_b = sb("ident_b", [P, P], BF16)
        before = sb("before", [P, P])
        ones = sb("ones", [P, P])
        neg_big = sb("neg_big", [P, 1])
        tiny_zero = sb("tiny_zero", [P, 1])
        coeff_t = sb("coeff_t", [pl.bases, pl.rel_b])
        wself_sb = sb("wself_sb", [D, D])
        bias_sb = sb("bias_sb", [P, D])
        beta_sb = sb("beta_sb", [P, 2])
        lane_bin = sb("lane_bin", [P, NB])
        bin_groups = sb("bin_groups", [P, NB])
        bin_groups_i = sb("bin_groups_i", [P, NB], I32)
        bin_first = sb("bin_first", [P, NB])
        bin_zero = sb("bin_zero", [P, NB])
        bin_from = sb("bin_from", [P, NB])
        first_col = sb("first_col", [NB, 1])
        reached = sb("reached", [NB, NG])
        block_s = sb("block_s", [1, NG], I32)
        block_d = sb("block_d", [1, NG], I32)

        idx = sb("idx", [P, RING, ITEMS], I32)
        hot_f = sb("hot_f", [P, 2, ITEMS, P])
        hot_t = sb("hot_t", [P, RING, ITEMS, P], BF16)
        pen_t = sb("pen_t", [P, 3, ITEMS * P], BF16)
        score = sb("score", [P, 3, ITEMS])
        score_b = sb("score_b", [P, 2, ITEMS], BF16)
        prod = sb("prod", [P, 2, ITEMS, D])
        dot = sb("dot", [P, 2, ITEMS])
        gmax = sb("gmax", [P, 2])
        new_max = sb("new_max", [P, 2], BF16)
        drop = sb("drop", [P, 2])
        keep = sb("keep", [P, 3, 2])
        shifted = sb("shifted", [P, 2, 2, ITEMS])
        less_src = sb("less_src", [P, 2, ITEMS])
        expd = sb("expd", [P, 2, 2, ITEMS])
        run_max = sb("run_max", [P, NB])
        out_sum = sb("out_sum", [P, NB])
        col_a = sb("col_a", [P, NB])
        col_b = sb("col_b", [P, NB])
        col_c = sb("col_c", [P, NB])
        h_blk = sb("h_blk", [P, 2, P])
        ht = sb("ht", [D, 2, P])

        pbig = ctx.enter_context(nc.psum_tensor("pbig", [P, 4, 512], F32))
        p_v = pbig[:, 2:4, :]
        p_t = pbig[:, 0:2, 0:256].bitcast(BF16)
        prow = ctx.enter_context(nc.psum_tensor("prow", [P, 2, 512], F32))
        p_row = prow[:, :, 0:ITEMS * D].rearrange("p s (j f) -> p s j f", j=ITEMS)
        p_max = ctx.enter_context(nc.psum_tensor("p_max", [P, 512], F32))
        p_sum = ctx.enter_context(nc.psum_tensor("p_sum", [P, 512], F32))
        p_cnt, p_col, p_turn = prow[:, 0, :], prow[:, 1, :], prow[:, :, 0:P]

        loaded_ids, loaded_w, loaded_types = sem("loaded_ids"), sem("loaded_w"), sem("loaded_types")
        loaded_basis, loaded_small = sem("loaded_basis"), sem("loaded_small")
        iota_made, consts_made = sem("iota_made"), sem("consts_made")
        relw_made, relw_kept, relw_stored = sem("relw_made"), sem("relw_kept"), sem("relw_stored")
        pads_made, pads_stored = sem("pads_made"), sem("pads_stored")
        counted, offsets_made, first_made, first_col_made = sem("counted"), sem("offsets_made"), sem("first_made"), sem("first_col_made")
        first_col_kept, reached_made, block_made = sem("first_col_kept"), sem("reached_made"), sem("block_made")
        blocks_ready = sem("blocks_ready")
        types_used = sem("types_used")
        pay_ready = sem("pay_ready")
        staged = [sem("staged0"), sem("staged1")]
        scattered = [sem("scattered0"), sem("scattered1")]
        scatters_started = sem("scatters_started")
        bins_loaded_s, bins_loaded_d = sem("bins_loaded_s"), sem("bins_loaded_d")
        x_cleared, x_loaded = sem("x_cleared"), sem("x_loaded")
        dve_step = sem("dve_step")
        dve_asks_act, act_answers = sem("dve_asks_act"), sem("act_answers")
        table_made, table_stored = sem("table_made"), sem("table_stored")
        units_made, sums_cleared = sem("units_made"), sem("sums_cleared")
        weights_loaded, h_made, out_made, out_stored = sem("weights_loaded"), sem("h_made"), sem("out_made"), sem("out_stored")
        blk_copied, blk_turned, ht_kept = sem("blk_copied"), sem("blk_turned"), sem("ht_kept")
        self_made, self_added = sem("self_made"), sem("self_added")
        chunk_made = [sem(f"chunk_made{k}") for k in range(4)]
        chunk_kept = [sem(f"chunk_kept{k}") for k in range(4)]
        chunk_stored = [sem(f"chunk_stored{k}") for k in range(4)]
        idx_ready = sem("idx_ready")
        gathers_started = sem("gathers_started")
        gathered = [sem(f"gathered{s}") for s in range(RING)]
        hot_made, turned, hot_t_made, pen_made = sem("hot_made"), sem("turned"), sem("hot_t_made"), sem("pen_made")
        hot_f_made, hot_f_direct = sem("hot_f_made"), sem("hot_f_direct")
        dst_rows, multiplied, dotted, scored, scored_b = sem("dst_rows"), sem("multiplied"), sem("dotted"), sem("scored"), sem("scored_b")
        spread, group_max, max_made, dropped, max_kept = sem("spread"), sem("group_max"), sem("max_made"), sem("dropped"), sem("max_kept")
        keep_made, edge_max, shift_made, exp_made = sem("keep_made"), sem("edge_max"), sem("shift_made"), sem("exp_made")
        unsourced = sem("unsourced")
        msg_made, summed, added = sem("msg_made"), sem("summed"), sem("added")

        def done(n):
            return n + 1 + CREDIT

        SOURCE, EDGE, AGNN, PLAIN = "source", "edge", "agnn", "plain"

        class Pass:
            def __init__(self, kind, every, gather, own, column=0, table=None):
                self.kind, self.column, self.table = kind, column, table
                self.every = every * NG
                self.gather = gather * NG
                self.nth = gather
                self.own = own * NG
                self.softmax = kind != PLAIN
                self.block = block_s if kind == SOURCE else block_d
                self.local = psf[:, :, 0] if kind == SOURCE else pdf[:, :, 1]
                self.weight = psf[:, :, 1] if kind == SOURCE else pdf[:, :, 2]

            def gathers(self, at):
                return self.nth * -(-(NG - at.slot) // RING) + at.rnd

        p_source = Pass(SOURCE, 0, 0, 0)
        p_edge = Pass(EDGE, 1, 0, 0, 0, tables[0])
        p_agnn = [Pass(AGNN, 2, 1, 0, 0, tables[1]), Pass(AGNN, 3, 2, 1, 0, tables[2])]
        p_plain = [Pass(PLAIN, 4, 3, 0, 3, table_a), Pass(PLAIN, 5, 4, 1, 4, table_b)]

        def run_pass(eng, steps):
            low, high = min(o for o, _ in steps), max(o for o, _ in steps)

            def turn(rnd, k):
                for off, step in steps:
                    step(At(rnd + (k + off) // RING, (k + off) % RING))

            def edge(i):
                for off, step in steps:
                    if 0 <= i + off < NG:
                        step(At((i + off) // RING, (i + off) % RING))

            first = -low
            rounds = (NG - high - first) // RING
            for i in range(-high, first):
                edge(i)
            with eng.Fori(0, rounds) as t:
                for k in range(RING):
                    turn(t, first + k)
            for i in range(first + RING * rounds, NG - low):
                edge(i)

        PER = [pl.rel_a * D // 512, pl.rel_b * D // 512]
        CB = [[0] * PER[0], [NB * (c < PER[0]) for c in range(PER[1])]]

        def over_blocks(eng, one):
            with eng.Fori(0, NB // 2) as t:
                for half in range(2):
                    one(t * 2 + half, half)
            if NB % 2:
                one(NB - 1, (NB - 1) % 2)

        block = ctx.enter_context(nc.Block())

        @block.sync
        def _(sp):
            def lanes(a):
                return a.rearrange("(p c) -> p c", c=COLS)

            sp.dma_start(src_c, lanes(src)).then_inc(loaded_ids, 16)
            sp.dma_start(dst_c, lanes(dst)).then_inc(loaded_ids, 16)
            sp.dma_start(wgt_c, lanes(weight)).then_inc(loaded_w, 16)
            sp.dma_start(typ_c, lanes(type_a)).then_inc(loaded_types, 16)
            sp.dma_start(basis_sb, basis.rearrange("b i o -> b (i o)")).then_inc(loaded_basis, 16)
            sp.dma_start(coeff_t[:, :], coeff.rearrange("r b -> b r"), allow_slow_non_contiguous=True).then_inc(loaded_basis, 16)
            sp.dma_start(wself_sb[:, :], w_self).then_inc(loaded_small, 16)
            sp.dma_start(bias_sb[:, :], bias.unsqueeze(0).to_broadcast([P, D])).then_inc(loaded_small, 16)
            sp.dma_start(beta_sb[:, :], beta.unsqueeze(0).to_broadcast([P, 2])).then_inc(loaded_small, 16)
            sp.wait_ge(relw_kept, 8)
            sp.dma_start(rel_w.rearrange("r i o -> r (i o)"), relw_sb).then_inc(relw_stored, 16)
            sp.wait_ge(pads_made, 1)
            sp.dma_start(bins_src.rearrange("(p n) f -> p (n f)", p=P), ps[:, 0:NI * 2]).then_inc(pads_stored, 16)
            sp.wait_ge(pads_made, 2)
            sp.dma_start(bins_dst.rearrange("(p n) f -> p (n f)", p=P), pd[:, 0:NI * 5]).then_inc(pads_stored, 16)
            sp.wait_ge(types_used, 1)
            sp.dma_start(typ_c, lanes(type_b)).then_inc(loaded_types, 16)

            def stage(pay, slot, s, t, uses):
                sp.wait_ge(scattered[s], (t + uses) * (16 * CH))
                sp.dma_start(slot[0:LANES, s, :, :], pay[:, bass.ds((t * 2 + s) * CH, CH), :]).then_inc(staged[s], 16)

            sp.wait_ge(pay_ready, 1)
            with sp.Fori(0, pl.stages) as t:
                for s in range(2):
                    stage(pays, slot_s, s, t, 0)
            for s in range(2):
                sp.wait_ge(scattered[s], pl.stages * 16 * CH)
            sp.dma_start(ps[:, 0:NI * 2], bins_src.rearrange("(p n) f -> p (n f)", p=P)).then_inc(bins_loaded_s, 16)
            sp.wait_ge(pay_ready, 2)
            sp.wait_ge(x_cleared, 1)
            sp.dma_start(x_sb[:, 0:FULL, :], x[0:FULL * P, :].rearrange("(b p) f -> p b f", p=P)).then_inc(x_loaded, 16)
            if FULL < NB:
                sp.dma_start(x_sb[0:pl.last, FULL, :], x[FULL * P:, :]).then_inc(x_loaded, 16)
            sp.wait_ge(relw_stored, 16)
            sp.dma_start(wa_sb.rearrange("i (r o) -> i r o", o=D), w_a.rearrange("r i o -> i r o")).then_inc(weights_loaded, 16)
            sp.dma_start(wb_sb.rearrange("i (r o) -> i r o", o=D), rel_w.rearrange("r i o -> i r o")).then_inc(weights_loaded, 16)
            with sp.Fori(0, pl.stages) as t:
                for s in range(2):
                    stage(payd, slot_d, s, t, pl.stages)
            for s in range(2):
                sp.wait_ge(scattered[s], 2 * pl.stages * 16 * CH)
            sp.dma_start(pd[:, 0:NI * 5], bins_dst.rearrange("(p n) f -> p (n f)", p=P)).then_inc(bins_loaded_d, 16)
            for k in range(3):
                sp.wait_ge(table_made, k + 1)
                sp.dma_start(tables[k].rearrange("(b p) f -> p b f", p=P), tab).then_inc(table_stored, 16)

            for k, table in enumerate((table_a, table_b)):
                view = table.rearrange("(b p r) f -> b p (r f)", p=P, b=NB)
                with sp.Fori(0, NB) as b:
                    for c in range(PER[k]):
                        sp.wait_ge(chunk_kept[c], CB[k][c] + b + 1)
                        sp.dma_start(view[b, :, c * 512:(c + 1) * 512], stg[:, c, :]).then_inc(chunk_stored[c], 16)
            sp.wait_ge(out_made, 1)
            sp.dma_start(out[0:FULL * P, :].rearrange("(b p) f -> p b f", p=P), x_sb[:, 0:FULL, :]).then_inc(out_stored, 16)
            if FULL < NB:
                sp.dma_start(out[FULL * P:, :], x_sb[0:pl.last, FULL, :]).then_inc(out_stored, 16)
            sp.wait_ge(out_stored, 16 * (1 + (FULL < NB)))

        @block.gpsimd
        def _(pool):
            pool.sem_inc(gathers_started, CREDIT)
            nc.gpsimd.iota(iota[:, :], pattern=[[1, 512]], base=0, channel_multiplier=0,
                           allow_small_or_imprecise_dtypes=True).then_inc(iota_made, 1)
            nc.gpsimd.iota(lane[:, :], pattern=[[0, 1]], base=0, channel_multiplier=1,
                           allow_small_or_imprecise_dtypes=True).then_inc(iota_made, 1)

            def scatter(bins, slot, words, s, t, uses):
                pool.wait_ge(staged[s], (t + uses + 1) * 16)
                pool.sem_inc(scatters_started, 1)
                for c in range(CH):
                    nc.gpsimd.indirect_dma_start(
                        bins, bass.IndirectOffsetOnAxis(ap=slot[0:LANES, s, c, words:words + 1], axis=0),
                        slot[0:LANES, s, c, 0:words], None).then_inc(scattered[s], 16)

            pool.wait_ge(pads_stored, 32)
            with pool.Fori(0, pl.stages) as t:
                for s in range(2):
                    scatter(bins_src, slot_s, 2, s, t, 0)
            with pool.Fori(0, pl.stages) as t:
                for s in range(2):
                    scatter(bins_dst, slot_d, 5, s, t, pl.stages)

            def gather(ps_):
                used = msg_made if ps_.softmax else summed
                width = ROW if ps_.softmax else D

                def fetch(at):
                    n = ps_.gather + at.g
                    u = at.g + (ps_.gather if ps_.softmax else ps_.every)
                    pool.wait_ge(idx_ready, done(n))
                    pool.wait_ge(used, done(u - RING))
                    pool.sem_inc(gathers_started, 1)
                    for j in range(ITEMS):
                        nc.gpsimd.indirect_dma_start(
                            rows[:, at.slot, j, 0:width], None, ps_.table,
                            bass.IndirectOffsetOnAxis(ap=idx[:, at.slot, j:j + 1], axis=0)).then_inc(gathered[at.slot], 16)
                run_pass(pool, [(0, fetch)])

            for k, ps_ in enumerate([p_edge] + p_agnn):
                pool.wait_ge(table_stored, 16 * (k + 1))
                gather(ps_)
            for k, ps_ in enumerate(p_plain):
                for c in range(PER[k]):
                    pool.wait_ge(chunk_stored[c], 16 * (CB[k][c] + NB))
                gather(ps_)

        @block.scalar
        def _(act):
            for s in (idx_ready, hot_t_made, pen_made, scored_b, keep_made, exp_made, ht_kept, hot_f_made):
                act.sem_inc(s, CREDIT)
            for k in range(8):
                act.wait_ge(relw_made, k + 1)
                nc.scalar.copy(relw_sb[:, k * 512:(k + 1) * 512], pbig[0:pl.rel_b, k % 4, :]).then_inc(relw_kept, 1)
            asked = [0]

            def root(col):
                asked[0] += 1
                act.wait_ge(dve_asks_act, asked[0])
                nc.scalar.activation(col, col, ACT.Sqrt).then_inc(act_answers, 1)

            def work(ps_):
                e = ps_.every

                def rows_wanted(at):
                    act.wait_ge(gathered[at.slot], ps_.gathers(at) * (16 * ITEMS))
                    nc.scalar.copy(idx[:, at.slot, :], pdi[:, bass.ds(at.g * ITEMS, ITEMS), ps_.column]).then_inc(idx_ready, 1)

                def turn_kept(at):
                    act.wait_ge(turned, done(e + at.g))
                    act.wait_ge(edge_max, done(e + at.g - RING))
                    nc.scalar.copy(hot_t[:, at.slot, :, :].rearrange("p j e -> p (j e)"), p_t[:, at.two, :]).then_inc(hot_t_made, 1)

                def penalty(at):
                    act.wait_ge(turned, done(e + at.g))
                    act.wait_ge(spread, done(e + at.g - 3))
                    nc.scalar.activation(pen_t[:, at.three, :], p_t[:, at.two, :], ACT.Identity,
                                         bias=neg_big[:, 0:1], scale=BIG).then_inc(pen_made, 1)

                def exponentials(at):
                    act.wait_ge(shift_made, done(e + at.g))
                    if ps_.kind == SOURCE:
                        act.wait_ge(summed, done(e + at.g - 2))
                    else:
                        act.wait_ge(msg_made, done(ps_.gather + at.g - 2))
                    if ps_.kind == EDGE:
                        nc.scalar.activation(expd[:, at.two, :, :], shifted[:, at.two, :, :], ACT.Exp).then_inc(exp_made, 1)
                    else:
                        nc.scalar.activation(expd[:, at.two, 0, :], shifted[:, at.two, 0, :], ACT.Exp).then_inc(exp_made, 1)

                def factors(at):
                    act.wait_ge(dropped, done(e + at.g))
                    act.wait_ge(added, done(e + at.g - 3))
                    last = nc.scalar.activation(keep[:, at.three, 0:1], drop[:, at.two:at.two + 1], ACT.Exp)
                    if ps_.kind == EDGE:
                        last = nc.scalar.activation(keep[:, at.three, 1:2], drop[:, at.two:at.two + 1], ACT.Exp, scale=0.5)
                    last.then_inc(keep_made, 1)

                def scores_rounded(at):
                    act.wait_ge(spread, done(e + at.g - 2))
                    if ps_.kind == AGNN:
                        act.wait_ge(scored, done(ps_.own + at.g))
                        nc.scalar.copy(score_b[:, at.two, :], score[:, at.three, :]).then_inc(scored_b, 1)
                    else:
                        nc.scalar.copy(score_b[:, at.two, :], ps_.weight[:, bass.ds(at.g * ITEMS, ITEMS)]).then_inc(scored_b, 1)

                def hot_widened(at):
                    act.wait_ge(hot_made, done(e + at.g))
                    act.wait_ge(summed, done(e + at.g - 2))
                    nc.scalar.copy(hot_f[:, at.two, :, :], hot[:, at.slot, :, :]).then_inc(hot_f_made, 1)

                steps = []
                if ps_.softmax:
                    steps += [(1, turn_kept), (-1, exponentials), (1, penalty), (0, factors),
                              (1, scores_rounded), (-1, hot_widened)]
                if ps_.kind != SOURCE:
                    steps += [(RING - 1, rows_wanted)]
                run_pass(act, steps)

            def build(k):
                def one(b, half):
                    n = k * NB + b
                    act.wait_ge(blk_turned, done(n))
                    act.wait_ge(chunk_made[PER[k] - 1], done(CB[k][-1] + b - 2))
                    nc.scalar.copy(ht[:, half, :], p_turn[0:D, half, :]).then_inc(ht_kept, 1)
                    for c in range(1, PER[k], 2):
                        act.wait_ge(chunk_made[c], done(CB[k][c] + b))
                        act.wait_ge(chunk_stored[c], (CB[k][c] + b) * 16)
                        nc.scalar.copy(stg[:, c, :], pbig[:, c, :]).then_inc(chunk_kept[c], 1)
                over_blocks(act, one)

            act.wait_ge(consts_made, 1)
            root(col_a[:, :])
            act.wait_ge(bins_loaded_s, 16)
            work(p_source)
            asked[0] += 1
            act.wait_ge(dve_asks_act, asked[0])
            nc.scalar.activation(col_b[:, :], col_b[:, :], ACT.Ln).then_inc(act_answers, 1)
            act.wait_ge(bins_loaded_d, 16)
            work(p_edge)
            root(col_a[:, :])
            root(col_a[:, :])
            root(col_a[:, :])
            work(p_agnn[0])
            root(col_a[:, :])
            work(p_agnn[1])

            root(col_a[:, :])
            build(0)
            work(p_plain[0])
            root(col_a[:, :])
            build(1)
            work(p_plain[1])

        @block.vector
        def _(dve):
            for s in (hot_made, hot_f_direct, multiplied, dotted, scored, group_max, max_made, dropped, max_kept,
                      shift_made, unsourced, msg_made, added, blk_copied, self_added):
                dve.sem_inc(s, CREDIT)
            steps = [0]

            def link(ins):
                steps[0] += 1
                ins.then_inc(dve_step, 1)
                dve.wait_ge(dve_step, steps[0])

            def linked(t, per, k):
                return steps[0] + t * per + k

            asked = [0]

            def ask(ins):
                asked[0] += 1
                ins.then_inc(dve_asks_act, 1)
                dve.wait_ge(act_answers, asked[0])

            v = nc.vector
            dve.wait_ge(iota_made, 2)
            v.tensor_scalar(ident[:, :], iota[:, 0:P], lane[:, 0:1], None, ALU.is_equal)
            v.tensor_scalar(ident_b[:, :], iota[:, 0:P], lane[:, 0:1], None, ALU.is_equal)
            v.tensor_scalar(before[:, :], iota[:, 0:P], lane[:, 0:1], None, ALU.is_gt)
            v.tensor_copy(iota_b[:, :], iota[:, 0:P])
            v.memset(ones[:, :], 1.0)
            v.memset(h_blk[:, :, :], 0.0)
            v.memset(bin_zero[:, :], 0.0)
            v.memset(run_max[:, :], -BIG)
            v.memset(out_sum[:, :], 0.0)
            link(v.memset(neg_big[:, :], -BIG))
            v.memset(lane_bin[:, :], 0.0).then_inc(consts_made, 1)
            v.memset(psf[:, :, 0], -1.0)
            v.memset(psf[:, :, 1], 0.0).then_inc(pads_made, 1)
            dve.wait_ge(relw_stored, 16)
            v.memset(pdi[:, :, 0], pl.nodes)
            v.memset(pdf[:, :, 1], -1.0)
            v.memset(pdf[:, :, 2], 0.0)
            v.memset(pdi[:, :, 3], pl.nodes * pl.rel_a)
            v.memset(pdi[:, :, 4], pl.nodes * pl.rel_b).then_inc(pads_made, 1)

            def sort(k, key, local, addr, blocks):
                link(v.tensor_scalar(hot_i, key, 7, None, ALU.arith_shift_right))
                link(v.tensor_copy(bin_c, hot_i))
                link(v.tensor_scalar(hot_i, key, 127, None, ALU.bitwise_and))
                link(v.tensor_copy(local, hot_i))
                with dve.Fori(0, NB) as b:
                    v.tensor_scalar(hot_c, bin_c, iota[0:LANES, bass.ds(b, 1)], None, ALU.is_equal, ALU.add,
                                    accum_out=lane_bin[0:LANES, bass.ds(b, 1)]).then_inc(dve_step, 1)
                    dve.wait_ge(dve_step, linked(b, 1, 1))
                steps[0] += NB
                v.engine_nop().then_inc(counted, 1)
                dve.wait_ge(offsets_made, k + 1)
                link(v.tensor_scalar(bin_groups_i[:, :], p_cnt[:, 64:64 + NB], float(ITEMS * P - 1), None, ALU.add))
                link(v.tensor_scalar(bin_groups_i[:, :], bin_groups_i[:, :], 9, None, ALU.arith_shift_right))
                link(v.tensor_copy(bin_groups[:, :], bin_groups_i[:, :]))
                link(v.tensor_tensor_scan(bin_first[:, :], bin_groups[:, :], bin_zero[:, :], 0.0, ALU.add, ALU.add))
                link(v.tensor_tensor(bin_first[:, :], bin_first[:, :], bin_groups[:, :], ALU.subtract))
                v.engine_nop().then_inc(first_made, 1)
                link(v.tensor_scalar(bin_from[:, :], bin_first[:, :], float(ITEMS * P), -1.0, ALU.mult, ALU.add))
                link(v.tensor_tensor(bin_from[0:LANES, :], bin_from[0:LANES, :], p_cnt[0:LANES, 0:NB], ALU.add))
                dve.wait_ge(first_col_made, k + 1)
                link(v.tensor_copy(first_col[:, :], p_col[0:NB, 0:1]))
                v.tensor_scalar(reached[:, :], iota[0:NB, 0:NG], first_col[:, 0:1], None, ALU.is_ge).then_inc(reached_made, 1)
                dve.wait_ge(block_made, k + 1)
                v.tensor_scalar(blocks[:, :], pbig[0:1, 0, 0:NG], -1.0, None, ALU.add).then_inc(blocks_ready, 1)
                link(v.memset(pos_c, 0.0))
                with dve.Fori(0, NB) as b:
                    v.tensor_scalar(hot_c, bin_c, iota[0:LANES, bass.ds(b, 1)], None, ALU.is_equal).then_inc(dve_step, 1)
                    dve.wait_ge(dve_step, linked(b, 4, 1))
                    v.tensor_tensor_scan(run_c, hot_c, hot_c, bin_from[0:LANES, bass.ds(b, 1)], ALU.add, ALU.bypass).then_inc(dve_step, 1)
                    dve.wait_ge(dve_step, linked(b, 4, 2))
                    v.tensor_tensor(hot_c, hot_c, run_c, ALU.mult).then_inc(dve_step, 1)
                    dve.wait_ge(dve_step, linked(b, 4, 3))
                    v.tensor_tensor(pos_c, pos_c, hot_c, ALU.add).then_inc(dve_step, 1)
                    dve.wait_ge(dve_step, linked(b, 4, 4))
                steps[0] += 4 * NB
                link(v.tensor_copy(hot_i, pos_c))
                link(v.tensor_scalar(run_i, hot_i, 127, None, ALU.bitwise_and))
                link(v.tensor_scalar(hot_i, hot_i, 7, None, ALU.arith_shift_right))
                link(v.scalar_tensor_tensor(out=addr, in0=run_i, scalar=float(NI), in1=hot_i, op0=ALU.mult, op1=ALU.add))

            dve.wait_ge(loaded_ids, 32)
            dve.wait_ge(loaded_w, 16)
            v.tensor_copy(paysf[:, :, 1], wgt_c)
            sort(0, src_c, paysf[:, :, 0], pays[:, :, 2], block_s)
            v.engine_nop().then_inc(pay_ready, 1)
            dve.wait_ge(loaded_types, 16)
            v.tensor_copy(payd[:, :, 0], src_c)
            v.tensor_copy(paydf[:, :, 2], wgt_c)
            v.scalar_tensor_tensor(out=payd[:, :, 3], in0=src_c, scalar=float(pl.rel_a), in1=typ_c,
                                   op0=ALU.mult, op1=ALU.add).then_inc(types_used, 1)
            sort(1, dst_c, paydf[:, :, 1], payd[:, :, 5], block_d)
            dve.wait_ge(loaded_types, 32)
            link(v.scalar_tensor_tensor(out=payd[:, :, 4], in0=src_c, scalar=float(pl.rel_b), in1=typ_c,
                                        op0=ALU.mult, op1=ALU.add))
            v.memset(x_sb[:, :, :], 0.0).then_inc(x_cleared, 1)
            v.engine_nop().then_inc(pay_ready, 1)

            def bc(col, n=D):
                return col.unsqueeze(2).to_broadcast([P, NB, n])

            def layer_norm():
                link(v.reduce_sum(col_a[:, :], x_sb[:, :, :], AX))
                link(v.tensor_scalar(col_a[:, :], col_a[:, :], 1.0 / D, None, ALU.mult))
                link(v.tensor_tensor(h_sb[:, :, :], x_sb[:, :, :], bc(col_a[:, :]), ALU.subtract))
                link(v.tensor_tensor(sq[:, :, :], h_sb[:, :, :], h_sb[:, :, :], ALU.mult))
                link(v.reduce_sum(col_a[:, :], sq[:, :, :], AX))
                ask(v.tensor_scalar(col_a[:, :], col_a[:, :], 1.0 / D, LN_EPS, ALU.mult, ALU.add))
                link(v.reciprocal(col_a[:, :], col_a[:, :]))
                link(v.tensor_tensor(h_sb[:, :, :], h_sb[:, :, :], bc(col_a[:, :]), ALU.mult))
                link(v.tensor_scalar(h_sb[:, :, :], h_sb[:, :, :], 0.0, None, ALU.max))

            def agnn_table(k):
                link(v.tensor_tensor(sq[:, :, :], h_sb[:, :, :], h_sb[:, :, :], ALU.mult))
                ask(v.reduce_sum(col_a[:, :], sq[:, :, :], AX))
                link(v.tensor_scalar(col_a[:, :], col_a[:, :], NORM_EPS, None, ALU.max))
                link(v.reciprocal(col_a[:, :], col_a[:, :]))
                link(v.tensor_tensor(sq[:, :, :], h_sb[:, :, :], bc(col_a[:, :]), ALU.mult))
                for part in range(3):
                    link(v.tensor_copy(unit3[:, part, :, :], sq[:, :, :]))
                    if part < 2:
                        link(v.tensor_tensor(sq[:, :, :], sq[:, :, :], unit3[:, part, :, :], ALU.subtract))
                v.engine_nop().then_inc(units_made, 1)
                v.tensor_scalar(tab[:, :, D], col_a[:, :], beta_sb[:, k:k + 1], None, ALU.mult)
                v.tensor_copy(tab[:, :, 0:D], h_sb[:, :, :]).then_inc(table_made, 1)

            def clear_sums():
                v.memset(run_max[:, :], -BIG)
                link(v.memset(acc[:, :, :], 0.0))

            def work(ps_):
                e = ps_.every

                def block_of(at):
                    return dve.value_load(ps_.block[0:1, bass.ds(at.g, 1)], min_val=0, max_val=NB - 1)

                def items(a, at):
                    return a[:, bass.ds(at.g * ITEMS, ITEMS)]

                def one_hots(at):
                    nodes = items(ps_.local, at).unsqueeze(2).to_broadcast([P, ITEMS, P])
                    if ps_.softmax:
                        dve.wait_ge(hot_f_made, done(e + at.g - RING))
                        v.tensor_tensor(hot[:, at.slot, :, :], iota_b[:, :].unsqueeze(1).to_broadcast([P, ITEMS, P]),
                                        nodes, ALU.is_equal).then_inc(hot_made, 1)
                    else:
                        dve.wait_ge(summed, done(e + at.g - 2))
                        v.tensor_tensor(hot_f[:, at.two, :, :], iota[:, 0:P].unsqueeze(1).to_broadcast([P, ITEMS, P]),
                                        nodes, ALU.is_equal).then_inc(hot_f_direct, 1)

                def scores(at):
                    a = ps_.own + at.g
                    here = rows[:, at.slot, :, :]
                    dve.wait_ge(gathered[at.slot], (ps_.gathers(at) + 1) * (16 * ITEMS))
                    dve.wait_ge(dst_rows, done(a))
                    dve.wait_ge(dotted, done(a - 2))
                    v.tensor_tensor(prod[:, at.two, :, :], here[:, :, 0:D], p_row[:, at.two, :, :], ALU.mult).then_inc(multiplied, 1)
                    dve.wait_ge(multiplied, done(a))
                    v.reduce_sum(dot[:, at.two, :], prod[:, at.two, :, :], AX).then_inc(dotted, 1)
                    dve.wait_ge(dotted, done(a))
                    dve.wait_ge(shift_made, done(e + at.g - 3))
                    v.tensor_tensor(score[:, at.three, :], dot[:, at.two, :], here[:, :, D], ALU.mult).then_inc(scored, 1)

                def maxima(at):
                    two = slice(at.two, at.two + 1)
                    b = block_of(at)
                    kept = run_max[:, bass.ds(b, 1)]
                    dve.wait_ge(spread, done(e + at.g))
                    v.reduce_max(gmax[:, two], p_v[:, at.two, :], AX).then_inc(group_max, 1)
                    dve.wait_ge(group_max, done(e + at.g))
                    dve.wait_ge(max_kept, done(e + at.g - 1))
                    dve.wait_ge(edge_max, done(e + at.g - 2))
                    v.tensor_tensor(new_max[:, two], kept, gmax[:, two], ALU.max).then_inc(max_made, 1)
                    dve.wait_ge(max_made, done(e + at.g))
                    dve.wait_ge(keep_made, done(e + at.g - 2))
                    v.tensor_tensor(drop[:, two], kept, new_max[:, two], ALU.subtract).then_inc(dropped, 1)
                    dve.wait_ge(dropped, done(e + at.g))
                    v.tensor_scalar(kept, new_max[:, two], 1.0, None, ALU.mult).then_inc(max_kept, 1)

                def less_maxima(at):
                    two = at.two
                    dve.wait_ge(exp_made, done(e + at.g - 2))
                    if ps_.kind == EDGE:
                        dve.wait_ge(gathered[at.slot], (ps_.gathers(at) + 1) * (16 * ITEMS))
                        v.tensor_tensor(less_src[:, two, :], items(ps_.weight, at), rows[:, at.slot, :, D], ALU.subtract).then_inc(unsourced, 1)
                    dve.wait_ge(edge_max, done(e + at.g))
                    if ps_.kind == AGNN:
                        dve.wait_ge(scored, done(ps_.own + at.g))
                        v.tensor_tensor(shifted[:, two, 0, :], score[:, at.three, :], p_max[:, 0:ITEMS], ALU.subtract).then_inc(shift_made, 1)
                    elif ps_.kind == SOURCE:
                        v.tensor_tensor(shifted[:, two, 0, :], items(ps_.weight, at), p_max[:, 0:ITEMS], ALU.subtract).then_inc(shift_made, 1)
                    else:
                        v.tensor_tensor(shifted[:, two, 0, :], items(ps_.weight, at), p_max[:, 0:ITEMS], ALU.subtract)
                        dve.wait_ge(unsourced, done(at.g))
                        v.scalar_tensor_tensor(out=shifted[:, two, 1, :], in0=p_max[:, 0:ITEMS], scalar=-0.5,
                                               in1=less_src[:, two, :], op0=ALU.mult, op1=ALU.add).then_inc(shift_made, 1)

                def messages(at):
                    dve.wait_ge(exp_made, done(e + at.g))
                    dve.wait_ge(summed, done(e + at.g - 2))
                    v.tensor_copy(msg[:, at.two, :, D], expd[:, at.two, 0, :])
                    v.tensor_tensor(msg[:, at.two, :, 0:D], rows[:, at.slot, :, 0:D],
                                    expd[:, at.two, int(ps_.kind == EDGE), :].unsqueeze(2).to_broadcast([P, ITEMS, D]),
                                    ALU.mult).then_inc(msg_made, 1)

                def sums(at):
                    b = block_of(at)
                    dve.wait_ge(summed, done(e + at.g))
                    dve.wait_ge(added, done(e + at.g - 1))
                    if ps_.softmax:
                        dve.wait_ge(keep_made, done(e + at.g))
                    keep_1, keep_half = keep[:, at.three, 0:1], keep[:, at.three, 1:2]
                    if ps_.kind == SOURCE:
                        v.scalar_tensor_tensor(out=out_sum[:, bass.ds(b, 1)], in0=out_sum[:, bass.ds(b, 1)], scalar=keep_1,
                                               in1=p_sum[:, 0:1], op0=ALU.mult, op1=ALU.add).then_inc(added, 1)
                    elif ps_.kind == EDGE:
                        v.scalar_tensor_tensor(out=acc[:, b, 0:D], in0=acc[:, b, 0:D], scalar=keep_half,
                                               in1=p_sum[:, 0:D], op0=ALU.mult, op1=ALU.add)
                        v.scalar_tensor_tensor(out=acc[:, b, D:ROW], in0=acc[:, b, D:ROW], scalar=keep_1,
                                               in1=p_sum[:, D:ROW], op0=ALU.mult, op1=ALU.add).then_inc(added, 1)
                    elif ps_.kind == AGNN:
                        v.scalar_tensor_tensor(out=acc[:, b, :], in0=acc[:, b, :], scalar=keep_1,
                                               in1=p_sum[:, 0:ROW], op0=ALU.mult, op1=ALU.add).then_inc(added, 1)
                    else:
                        v.tensor_tensor(acc[:, b, :], acc[:, b, :], p_sum[:, 0:ROW], ALU.add).then_inc(added, 1)

                if ps_.kind == PLAIN:
                    run_pass(dve, [(1, one_hots), (-1, sums)])
                elif ps_.kind == SOURCE:
                    run_pass(dve, [(-1, less_maxima), (3, one_hots), (0, maxima), (-2, sums)])
                elif ps_.kind == EDGE:
                    run_pass(dve, [(-1, less_maxima), (3, one_hots), (0, maxima), (-1, messages), (-2, sums)])
                else:
                    run_pass(dve, [(-1, less_maxima), (3, one_hots), (0, maxima), (-1, messages), (1, scores), (-2, sums)])
                dve.wait_ge(added, done(e + NG - 1))

            def build(k):
                def one(b, half):
                    n = k * NB + b
                    dve.wait_ge(blk_turned, done(n - 2))
                    v.tensor_scalar(h_blk[:, half, 0:D], h_sb[:, b, :], 1.0, None, ALU.mult).then_inc(blk_copied, 1)
                    for c in range(0, PER[k], 2):
                        dve.wait_ge(chunk_made[c], done(CB[k][c] + b))
                        dve.wait_ge(chunk_stored[c], (CB[k][c] + b) * 16)
                        v.tensor_copy(stg[:, c, :], pbig[:, c, :]).then_inc(chunk_kept[c], 1)
                    if k == 1:
                        dve.wait_ge(self_made, done(b))
                        v.tensor_tensor(x_sb[:, b, :], x_sb[:, b, :], p_sum[:, 0:D], ALU.add).then_inc(self_added, 1)
                over_blocks(dve, one)

            for _ in range(1):
                dve.wait_ge(x_loaded, 16 * (1 + (FULL < NB)))
                layer_norm()
            dve.wait_ge(bins_loaded_s, 16)
            work(p_source)
            link(v.tensor_scalar(col_b[:, :], out_sum[:, :], 2.0 ** -60, None, ALU.max))
            link(v.tensor_scalar(col_c[:, :], out_sum[:, :], 2.0 ** -59, 0.5, ALU.is_gt, ALU.mult))
            ask(v.engine_nop())
            link(v.tensor_tensor(col_b[:, :], col_b[:, :], run_max[:, :], ALU.add))
            link(v.tensor_tensor(tab[:, :, D], col_b[:, :], col_c[:, :], ALU.mult))
            v.tensor_copy(tab[:, :, 0:D], h_sb[:, :, :]).then_inc(table_made, 1)
            dve.wait_ge(bins_loaded_d, 16)
            clear_sums()
            work(p_edge)
            link(v.tensor_scalar(col_a[:, :], acc[:, :, D], 1e-30, None, ALU.max))
            ask(v.engine_nop())
            link(v.reciprocal(col_a[:, :], col_a[:, :]))
            link(v.tensor_tensor(acc[:, :, 0:D], acc[:, :, 0:D], bc(col_a[:, :]), ALU.mult))
            link(v.tensor_tensor(x_sb[:, :, :], x_sb[:, :, :], acc[:, :, 0:D], ALU.add))

            layer_norm()
            dve.wait_ge(loaded_small, 48)
            for k in range(2):
                agnn_table(k)
                clear_sums()
                work(p_agnn[k])
                link(v.tensor_scalar(col_a[:, :], acc[:, :, D], 1e-30, None, ALU.max))
                link(v.reciprocal(col_a[:, :], col_a[:, :]))
                link(v.tensor_tensor(h_sb[:, :, :], acc[:, :, 0:D], bc(col_a[:, :]), ALU.mult))
                link(v.tensor_scalar(h_sb[:, :, :], h_sb[:, :, :], 0.0, None, ALU.max))
            link(v.tensor_tensor(x_sb[:, :, :], x_sb[:, :, :], h_sb[:, :, :], ALU.add))

            layer_norm()
            dve.wait_ge(weights_loaded, 32)
            build(0)
            v.memset(rows[:, :, :, D], 1.0)
            clear_sums()
            work(p_plain[0])
            link(v.tensor_tensor(x_sb[:, :, :], x_sb[:, :, :], acc[:, :, 0:D], ALU.add))

            layer_norm()
            link(v.tensor_tensor(x_sb[:, :, :], x_sb[:, :, :], bias_sb[:, :].unsqueeze(1).to_broadcast([P, NB, D]), ALU.add))
            build(1)
            clear_sums()
            work(p_plain[1])
            link(v.tensor_scalar(col_a[:, :], acc[:, :, D], 1.0, None, ALU.max))
            link(v.reciprocal(col_a[:, :], col_a[:, :]))
            link(v.tensor_tensor(acc[:, :, 0:D], acc[:, :, 0:D], bc(col_a[:, :]), ALU.mult))
            v.tensor_tensor(x_sb[:, :, :], x_sb[:, :, :], acc[:, :, 0:D], ALU.add).then_inc(out_made, 1)

        @block.tensor
        def _(pe):
            for s in (turned, dst_rows, spread, edge_max, summed, blk_turned, self_made, *chunk_made):
                pe.sem_inc(s, CREDIT)
            mm = nc.tensor.matmul
            pe.wait_ge(loaded_basis, 32)
            for k in range(8):
                if k >= 4:
                    pe.wait_ge(relw_kept, k - 3)
                mm(pbig[0:pl.rel_b, k % 4, :], coeff_t[:, :], basis_sb[:, k * 512:(k + 1) * 512],
                   start=True, stop=True).then_inc(relw_made, 1)
            pe.wait_ge(consts_made, 1)
            pe.wait_ge(relw_kept, 8)
            for k in range(2):
                pe.wait_ge(counted, k + 1)
                mm(p_cnt[0:LANES, 0:NB], before[0:LANES, 0:LANES], lane_bin[0:LANES, :], start=True, stop=True)
                mm(p_cnt[:, 64:64 + NB], ones[0:LANES, :], lane_bin[0:LANES, :], start=True, stop=True).then_inc(offsets_made, 1)
                pe.wait_ge(first_made, k + 1)
                mm(p_col[0:NB, 0:1], bin_first[0:1, :], ones[0:1, 0:1], start=True, stop=True).then_inc(first_col_made, 1)
                pe.wait_ge(reached_made, k + 1)
                mm(pbig[0:1, 0, 0:NG], ones[0:NB, 0:1], reached[:, :], start=True, stop=True).then_inc(block_made, 1)

            def work(ps_):
                e = ps_.every

                def turned_hots(at):
                    pe.wait_ge(hot_made, done(e + at.g))
                    pe.wait_ge(pen_made, done(e + at.g - 2))
                    for j in range(ITEMS):
                        last = nc.tensor.transpose(p_t[:, at.two, j * P:(j + 1) * P], hot[:, at.slot, j, :], ident_b[:, :])
                    last.then_inc(turned, 1)

                def rows_of_destinations(at):
                    b = pe.value_load(ps_.block[0:1, bass.ds(at.g, 1)], min_val=0, max_val=NB - 1)
                    pe.wait_ge(hot_t_made, done(e + at.g))
                    pe.wait_ge(multiplied, done(ps_.own + at.g - 2))
                    for j in range(ITEMS):
                        for part in range(3):
                            last = mm(p_row[:, at.two, j, :], hot_t[:, at.slot, j, :], unit3[:, part, b, :],
                                      start=part == 0, stop=part == 2)
                    last.then_inc(dst_rows, 1)

                def spread_scores(at):
                    pe.wait_ge(pen_made, done(e + at.g))
                    pe.wait_ge(group_max, done(e + at.g - 2))
                    mm(p_v[:, at.two, :], ident_b[:, :], pen_t[:, at.three, :], start=True, stop=False)
                    pe.wait_ge(scored_b, done(e + at.g))
                    for j in range(ITEMS):
                        last = mm(p_v[:, at.two, j * P:(j + 1) * P], score_b[:, at.two, j:j + 1].to_broadcast([P, P]),
                                  ident_b[:, :], start=False, stop=j == ITEMS - 1)
                    last.then_inc(spread, 1)

                def maxima_of_edges(at):
                    pe.wait_ge(max_made, done(e + at.g))
                    pe.wait_ge(hot_t_made, done(e + at.g))
                    pe.wait_ge(shift_made, done(e + at.g - 1))
                    for j in range(ITEMS):
                        last = mm(p_max[:, j:j + 1], hot_t[:, at.slot, j, :], new_max[:, at.two:at.two + 1],
                                  start=True, stop=True)
                    last.then_inc(edge_max, 1)

                def sums_per_node(at):
                    pe.wait_ge(added, done(e + at.g - 1))
                    if ps_.softmax:
                        pe.wait_ge(hot_f_made, done(e + at.g))
                    else:
                        pe.wait_ge(hot_f_direct, done(ps_.own + at.g))
                    if ps_.kind == SOURCE:
                        pe.wait_ge(exp_made, done(e + at.g))
                    elif ps_.softmax:
                        pe.wait_ge(msg_made, done(ps_.gather + at.g))
                    else:
                        pe.wait_ge(gathered[at.slot], (ps_.gathers(at) + 1) * (16 * ITEMS))
                    for j in range(ITEMS):
                        if ps_.kind == SOURCE:
                            given = expd[:, at.two, 0, j:j + 1]
                        elif ps_.softmax:
                            given = msg[:, at.two, j, :]
                        else:
                            given = rows[:, at.slot, j, :]
                        last = mm(p_sum[:, 0:given.shape[1]], hot_f[:, at.two, j, :], given,
                                  start=j == 0, stop=j == ITEMS - 1)
                    last.then_inc(summed, 1)

                if ps_.kind == PLAIN:
                    run_pass(pe, [(0, sums_per_node)])
                elif ps_.kind == AGNN:
                    run_pass(pe, [(-1, maxima_of_edges), (0, spread_scores), (1, rows_of_destinations),
                                  (-2, sums_per_node), (2, turned_hots)])
                else:
                    run_pass(pe, [(-1, maxima_of_edges), (0, spread_scores), (-2, sums_per_node), (2, turned_hots)])

            def build(k):
                weights = (wa_sb, wb_sb)[k]

                def one(b, half):
                    n = k * NB + b
                    pe.wait_ge(blk_copied, done(n))
                    pe.wait_ge(ht_kept, done(n - 2))
                    nc.tensor.transpose(p_turn[:, half, :], h_blk[:, half, :], ident[:, :]).then_inc(blk_turned, 1)
                    pe.wait_ge(ht_kept, done(n))
                    if k == 1:
                        pe.wait_ge(self_added, done(b - 1))
                        mm(p_sum[:, 0:D], ht[:, half, :], wself_sb[:, :], start=True, stop=True).then_inc(self_made, 1)
                    for c in range(PER[k]):
                        pe.wait_ge(chunk_kept[c], CB[k][c] + b)
                        mm(pbig[:, c, :], ht[:, half, :], weights[:, c * 512:(c + 1) * 512],
                           start=True, stop=True).then_inc(chunk_made[c], 1)
                over_blocks(pe, one)

            pe.wait_ge(blocks_ready, 1)
            work(p_source)
            pe.wait_ge(blocks_ready, 2)
            work(p_edge)
            for k in range(2):
                pe.wait_ge(units_made, k + 1)
                work(p_agnn[k])
            pe.wait_ge(weights_loaded, 32)
            build(0)
            work(p_plain[0])
            build(1)
            work(p_plain[1])


def kernel(x, src, dst, edge_type_16, edge_type_32, edge_weight, L1_gnn_beta, L2_gnn_weight,
           L3_gnn_basis, L3_gnn_coeff, L3_gnn_self_weight, L3_gnn_bias):
    import numpy as np
    import concourse.bacc as bacc
    from concourse.bass_utils import run_bass_kernel_spmd

    given = dict(x=x, src=src, dst=dst, type_a=edge_type_16, type_b=edge_type_32, weight=edge_weight,
                 beta=L1_gnn_beta, w_a=L2_gnn_weight, basis=L3_gnn_basis, coeff=L3_gnn_coeff,
                 w_self=L3_gnn_self_weight, bias=L3_gnn_bias)
    nc = bacc.Bacc("TRN2", target_bir_lowering=False, num_devices=1)
    arrays, args = {}, []
    for name, a in given.items():
        a = np.ascontiguousarray(a)
        arrays[f"in_{name}"] = a
        args.append(nc.dram_tensor(f"in_{name}", a.shape, mybir.dt.from_np(a.dtype), kind="ExternalInput").ap())
    out = nc.dram_tensor("out", np.shape(x), F32, kind="ExternalOutput").ap()
    gnn_program(nc, *args, out)
    r = run_bass_kernel_spmd(nc, [arrays], core_ids=[0])
    return r.results[0]["out"]
```

```python
import concourse.bass as bass
from concourse import mybir
from contextlib import ExitStack

F32 = mybir.dt.float32
BF16 = mybir.dt.bfloat16
I32 = mybir.dt.int32
ALU = mybir.AluOpType
ACT = mybir.ActivationFunctionType
AX = mybir.AxisListType.X

P = 128
ITEMS = 3
RING = 6
CREDIT = 8
D = 64
ROW = D + 1
BIG = float(2 ** 100)
LN_EPS = 1e-5
NORM_EPS = 1e-12
RANGE = 40.0


class Plan:

    def __init__(self, nodes, edges, rel_a, rel_b, bases):
        self.nodes, self.edges = nodes, edges
        self.rel_a, self.rel_b, self.bases = rel_a, rel_b, bases
        self.blocks = -(-nodes // P)
        self.last = nodes - (self.blocks - 1) * P
        self.lanes = max(d for d in range(1, P + 1) if edges % d == 0)
        self.cols = edges // self.lanes
        self.stage = max(c for c in range(1, 21) if self.cols % (2 * c) == 0)
        self.stages = self.cols // (2 * self.stage)
        ends = [min(3, self.stages), min(8, self.stages)]
        while ends[-1] < self.stages:
            ends.append(min(ends[-1] + 12, self.stages))
        self.ends = sorted(set(ends))
        assert self.ends[0] > 1
        self.piece = max(c for c in range(1, 7) if self.cols % c == 0)
        most = (edges + self.blocks * (ITEMS * P - 1)) // (ITEMS * P)
        self.groups = most
        self.items = self.groups * ITEMS
        self.ratio, self.shift = -(-2048 // ITEMS), 11
        assert all(n * self.ratio >> self.shift == n // ITEMS for n in range(edges // P + ITEMS + 2))
        assert self.last < P, "a row behind the last node serves the padding"


class At:

    def __init__(self, rnd, slot, ring=RING):
        self.rnd, self.slot = rnd, slot
        self.two, self.three = slot % 2, slot % 3
        self.g = rnd * ring + slot


def gnn_program(nc, x, src, dst, type_a, type_b, weight, beta, w_a, basis, coeff, w_self, bias, out):
    pl = Plan(x.shape[0], src.shape[0], w_a.shape[0], coeff.shape[0], basis.shape[0])
    NB, LANES, COLS, NI, NG = pl.blocks, pl.lanes, pl.cols, pl.items, pl.groups
    CH = pl.stage
    FULL = NB - 1 if pl.last < P else NB

    def scratch(name, shape, dt=F32):
        return nc.dram_tensor(name, shape, dt).ap()

    bins = scratch("bins", (P * NI, 5), I32)
    tables = [scratch(f"table{k}", (NB * P, ROW)) for k in range(3)]
    table_a = scratch("table_a", (NB * P * pl.rel_a, D))
    table_b = scratch("table_b", (NB * P * pl.rel_b, D))
    rel_w = scratch("rel_w", (pl.rel_b, D, D))

    ctx = ExitStack()
    with ctx:
        def sb(name, shape, dt=F32):
            return ctx.enter_context(nc.sbuf_tensor(name, shape, dt))

        def sem(name):
            return ctx.enter_context(nc.semaphore(name))

        WCOLS = (pl.rel_a + pl.rel_b + 1) * D
        ZW = max(8 * COLS, 2 * NB * D + NB * ROW + (RING + 2) * ITEMS * ROW + max(RING * ITEMS * P // 2, NB * D),
                 2 * NB * D + WCOLS)
        Z = sb("Z", [P, ZW])
        pay = sb("pay", [P, max(COLS * 6, NB * ROW + max(3 * NB * D // 2, 8 * 512))], I32)
        PC = pl.piece
        weights = sb("weights", [P, max(3 * WCOLS // 2, COLS + 2 * PC * (P + NB))])
        pd = sb("pd", [P, max(NI * 5, 2 * D * D)], I32)

        def zcol(k, dt=F32):
            return Z[0:LANES, k * COLS:(k + 1) * COLS].bitcast(dt) if dt != F32 else Z[0:LANES, k * COLS:(k + 1) * COLS]

        src_c, dst_c, typ_c = zcol(0, I32), zcol(1, I32), zcol(2, I32)
        wgt_c, pos_c, tmp_c, run_c = zcol(3), zcol(5), zcol(6), zcol(7)
        bin_c, hot_c = zcol(4, BF16)[:, 0:COLS], zcol(4, BF16)[:, COLS:2 * COLS]
        tmp_i, run_i = zcol(6, I32), zcol(7, I32)
        payd = pay[0:LANES, 0:COLS * 6].rearrange("p (c f) -> p c f", f=6)
        paydf = pay[0:LANES, 0:COLS * 6].bitcast(F32).rearrange("p (c f) -> p c f", f=6)
        typ_b = weights[0:LANES, 0:COLS].bitcast(I32)
        o = COLS + 2 * PC * P
        low_hot = weights[0:LANES, COLS:o].rearrange("p (s c n) -> p s c n", s=2, c=PC)
        high_exp = weights[0:LANES, o:o + 2 * PC * NB].rearrange("p (s c n) -> p s c n", s=2, c=PC)
        low_c, high_c, exp_c, src_f = hot_c, bin_c, run_c, zcol(1)
        slots = sb("slots", [P, 2, CH, 6], I32)
        pdi = pd[:, 0:NI * 5].rearrange("p (n f) -> p n f", f=5)
        pdf = pd[:, 0:NI * 5].bitcast(F32).rearrange("p (n f) -> p n f", f=5)
        basis_sb = pd[0:pl.bases, 0:D * D].bitcast(F32)
        relw_sb = pd[0:pl.rel_b, D * D:2 * D * D].bitcast(F32)
        o = 0
        x_sb = Z[:, o:o + NB * D].rearrange("p (b f) -> p b f", f=D)
        o += NB * D
        h_sb = Z[:, o:o + NB * D].rearrange("p (b f) -> p b f", f=D)
        o += NB * D
        tab_flat = Z[:, o:o + NB * ROW]
        tab = tab_flat.rearrange("p (b f) -> p b f", f=ROW)
        sq = Z[:, o:o + NB * D].rearrange("p (b f) -> p b f", f=D)
        o += NB * ROW
        rows = Z[:, o:o + RING * ITEMS * ROW].rearrange("p (s j f) -> p s j f", s=RING, j=ITEMS)
        o += RING * ITEMS * ROW
        msg = Z[:, o:o + 2 * ITEMS * ROW].rearrange("p (s j f) -> p s j f", s=2, j=ITEMS)
        o += 2 * ITEMS * ROW
        hot = Z[:, o:o + RING * ITEMS * P // 2].bitcast(BF16).rearrange("p (s j n) -> p s j n", s=RING, j=ITEMS)
        unit = Z[:, o:o + NB * D].rearrange("p (b f) -> p b f", f=D)
        acc = pay[:, 0:NB * ROW].bitcast(F32).rearrange("p (b f) -> p b f", f=ROW)
        unit3 = pay[:, NB * ROW:NB * ROW + 3 * NB * D // 2].bitcast(BF16).rearrange("p (k b f) -> p k b f", k=3, f=D)
        stg = pay[:, NB * ROW:NB * ROW + 8 * 512].bitcast(F32).rearrange("p (s c) -> p s c", s=8)
        w_f32 = Z[:, 2 * NB * D:2 * NB * D + WCOLS]
        w_parts = weights[:, 0:3 * WCOLS // 2].bitcast(BF16).rearrange("p (k c) -> p k c", k=3)

        WIDE = max(512, NG)
        iota = sb("iota", [P, WIDE])
        iota_b = sb("iota_b", [P, P], BF16)
        lane = sb("lane", [P, 1])
        ident = sb("ident", [P, P])
        ident_b = sb("ident_b", [P, P], BF16)
        before = sb("before", [P, P])
        ones = sb("ones", [P, P])
        neg_big = sb("neg_big", [P, 1])
        coeff_t = sb("coeff_t", [pl.bases, pl.rel_b])
        bias_sb = sb("bias_sb", [P, D])
        beta_sb = sb("beta_sb", [P, 2])
        lane_bin = sb("lane_bin", [P, NB])
        bin_groups = sb("bin_groups", [P, NB])
        bin_groups_i = sb("bin_groups_i", [P, NB], I32)
        bin_first = sb("bin_first", [P, NB])
        bin_zero = sb("bin_zero", [P, NB])
        bin_from = sb("bin_from", [P, NB])
        first_col = sb("first_col", [NB, 1])
        reached = sb("reached", [NB, NG])
        extremes = sb("extremes", [P, 2])
        spread_of = sb("spread_of", [1, 3])
        wide = sb("wide", [1, 1], I32)
        guard = sb("guard", [P, 1])
        node_no = sb("node_no", [P, 2])
        cand = sb("cand", [P, P])
        node_max = sb("node_max", [P, P])
        block_max = sb("block_max", [P, 1])
        group_block = sb("group_block", [1, NG], I32)

        idx = sb("idx", [P, RING, ITEMS], I32)
        hot_f = sb("hot_f", [P, 2, ITEMS, P])
        hot_t = sb("hot_t", [P, RING, ITEMS, P], BF16)
        pen_t = sb("pen_t", [P, 3, ITEMS * P], BF16)
        score = sb("score", [P, 3, ITEMS])
        score_b = sb("score_b", [P, 2, ITEMS], BF16)
        prod = sb("prod", [P, 2, ITEMS, D])
        dot = sb("dot", [P, 2, ITEMS])
        gmax = sb("gmax", [P, 2])
        new_max = sb("new_max", [P, 2], BF16)
        rise = sb("rise", [P, 3])
        keep = sb("keep", [P, RING, 2])
        shifted = sb("shifted", [P, 2, 2, ITEMS])
        less_src = sb("less_src", [P, 2, ITEMS])
        expd = sb("expd", [P, 2, 2, ITEMS])
        run_max = sb("run_max", [P, NB])
        out_sum = sb("out_sum", [P, NB])
        col_a = sb("col_a", [P, NB])
        col_b = sb("col_b", [P, NB])
        col_c = sb("col_c", [P, NB])
        h_parts = sb("h_parts", [P, 2, 4 * D], BF16)
        h_rest = sb("h_rest", [P, 2, D])
        ht = sb("ht", [P, 2, 2 * P], BF16)

        pbig = ctx.enter_context(nc.psum_tensor("pbig", [P, 4, 512], F32))
        p_v = pbig[:, 2:4, :]
        p_t = pbig[:, 0:2, 0:256].bitcast(BF16)
        prow = ctx.enter_context(nc.psum_tensor("prow", [P, 2, 512], F32))
        p_row = prow[:, :, 0:ITEMS * D].rearrange("p s (j f) -> p s j f", j=ITEMS)
        p_max = ctx.enter_context(nc.psum_tensor("p_max", [P, 512], F32))
        p_sum = ctx.enter_context(nc.psum_tensor("p_sum", [P, 512], F32))
        p_cnt, p_col, p_turn = prow[:, 0, :], prow[:, 1, :], prow[:, :, 0:P].bitcast(BF16)

        loaded_dst, loaded_src, loaded_w, loaded_types = sem("loaded_dst"), sem("loaded_src"), sem("loaded_w"), sem("loaded_types")
        loaded_basis, loaded_small = sem("loaded_basis"), sem("loaded_small")
        iota_made, consts_made = sem("iota_made"), sem("consts_made")
        relw_made, relw_kept, relw_stored = sem("relw_made"), sem("relw_kept"), sem("relw_stored")
        padding_made, pads_stored = sem("padding_made"), sem("pads_stored")
        counted, offsets_made, first_made, first_col_made = sem("counted"), sem("offsets_made"), sem("first_made"), sem("first_col_made")
        reached_made, block_made = sem("reached_made"), sem("block_made")
        blocks_ready = sem("blocks_ready")
        pay_ready = sem("pay_ready")
        staged = [sem("staged0"), sem("staged1")]
        scattered = [sem("scattered0"), sem("scattered1")]
        scatters_started = sem("scatters_started")
        bins_loaded = sem("bins_loaded")
        x_cleared, x_loaded = sem("x_cleared"), sem("x_loaded")
        extremes_made, extremes_turned, wide_made, guard_spread = sem("extremes_made"), sem("extremes_turned"), sem("wide_made"), sem("guard_spread")
        less_guard, exps_made = sem("less_guard"), sem("exps_made")
        high_made, piece_made, piece_used, out_summed = sem("high_made"), sem("piece_made"), sem("piece_used"), sem("out_summed")
        wide_set, masked, joined, numbered, reduced = sem("wide_set"), sem("masked"), sem("joined"), sem("numbered"), sem("reduced")
        cand_made, cand_turned, block_max_made, node_max_spread, node_max_kept = sem("cand_made"), sem("cand_turned"), sem("block_max_made"), sem("node_max_spread"), sem("node_max_kept")
        taken, numbered_2, lessened = sem("taken"), sem("numbered_2"), sem("lessened")
        dve_step = sem("dve_step")
        dve_asks_act, act_answers = sem("dve_asks_act"), sem("act_answers")
        table_made, table_stored = sem("table_made"), sem("table_stored")
        units_made = sem("units_made")
        weights_loaded, weights_split = sem("weights_loaded"), sem("weights_split")
        out_made, out_stored = sem("out_made"), sem("out_stored")
        blk_high, blk_less, blk_mid, blk_split = sem("blk_high"), sem("blk_less"), sem("blk_mid"), sem("blk_split")
        blk_turned, ht_kept = sem("blk_turned"), sem("ht_kept")
        self_made, self_added = sem("self_made"), sem("self_added")
        chunk_made = [sem(f"chunk_made{k}") for k in range(4)]
        chunk_kept = [sem(f"chunk_kept{k}") for k in range(4)]
        chunk_stored = [sem(f"chunk_stored{k}") for k in range(8)]
        idx_ready = sem("idx_ready")
        gathers_started = sem("gathers_started")
        gathered = [sem(f"gathered{s}") for s in range(RING)]
        hot_made, turned, hot_t_made, pen_made = sem("hot_made"), sem("turned"), sem("hot_t_made"), sem("pen_made")
        hot_f_made, hot_f_direct = sem("hot_f_made"), sem("hot_f_direct")
        dst_rows, multiplied, dotted, scored, scored_b = sem("dst_rows"), sem("multiplied"), sem("dotted"), sem("scored"), sem("scored_b")
        spread, group_max, max_made, risen, max_kept = sem("spread"), sem("group_max"), sem("max_made"), sem("risen"), sem("max_kept")
        keep_made, edge_max, shift_made, exp_made = sem("keep_made"), sem("edge_max"), sem("shift_made"), sem("exp_made")
        unsourced = sem("unsourced")
        msg_made, summed, added = sem("msg_made"), sem("summed"), sem("added")

        def done(n):
            return n + 1 + CREDIT

        EDGE, AGNN, PLAIN = "edge", "agnn", "plain"

        class Pass:
            def __init__(self, kind, every, gather, own, column=0, table=None):
                self.kind, self.column, self.table = kind, column, table
                self.every = every * NG
                self.gather = gather * NG
                self.nth = gather
                self.own = own * NG
                self.softmax = kind != PLAIN
                self.block, self.local, self.weight = group_block, pdf[:, :, 1], pdf[:, :, 2]

            def gathers(self, at):
                return self.nth * -(-(NG - at.slot) // RING) + at.rnd

        p_edge = Pass(EDGE, 0, 0, 0, 0, tables[0])
        p_agnn = [Pass(AGNN, 1, 1, 0, 0, tables[1]), Pass(AGNN, 2, 2, 1, 0, tables[2])]
        p_plain = [Pass(PLAIN, 3, 3, 0, 3, table_a), Pass(PLAIN, 4, 4, 1, 4, table_b)]

        def run_pass(eng, steps, blocks=None, wanted=(0, 0), count=NG, ring=RING):
            low, high = min(o for o, _ in steps), max(o for o, _ in steps)
            first = -low
            rounds = (count - high - first) // ring

            def read(start, n):
                return nc.values_load_multi_w_load_instructions(
                    blocks[0:1, bass.ds(start, n)], engines=[eng.engine], min_val=0, max_val=NB - 1,
                    skip_runtime_bounds_check_because="a count of bins, less one")[1]

            def edge(turns):
                base = max(turns.start + wanted[0], 0)
                n = min(turns.stop - 1 + wanted[1], count - 1) - base + 1
                known = read(base, n) if blocks is not None and n > 0 else ()
                for i in turns:
                    for off, step in steps:
                        g = i + off
                        if 0 <= g < count:
                            at = At(g // ring, g % ring, ring)
                            if base <= g < base + len(known):
                                at.block = known[g - base]
                            step(at)

            edge(range(-high, first))
            with eng.Fori(0, rounds) as t:
                if blocks is not None:
                    known = read(t * ring + (first + wanted[0]), ring + wanted[1] - wanted[0])
                for k in range(ring):
                    for off, step in steps:
                        g = first + k + off
                        at = At(t + g // ring, g % ring, ring)
                        if blocks is not None and wanted[0] <= off <= wanted[1]:
                            at.block = known[k + off - wanted[0]]
                        step(at)
            rest = range(first + ring * rounds, count - low)
            for i in range(0, len(rest), ring):
                edge(rest[i:i + ring])

        PER = [pl.rel_a * D // 512, pl.rel_b * D // 512]
        CB = [[0] * PER[0], [NB * (c < PER[0]) for c in range(PER[1])]]
        BANKS = [4 // PER[0], 4 // PER[1]]
        ON_DVE = [(), (1,)]

        def bank(k, at, c):
            return at.slot % BANKS[k] * PER[k] + c

        def blocks_of(parity):
            return (NB + 1 - parity) // 2

        def stores_before(k, slot):
            return blocks_of(slot // PER[0]) if k == 1 and slot < 2 * PER[0] else 0

        def copy_piece(eng, copy, k, at, c):
            slot = at.slot * PER[k] + c
            eng.wait_ge(chunk_made[c], done(CB[k][c] + at.g))
            eng.wait_ge(chunk_stored[slot], (stores_before(k, slot) + at.rnd) * 16 + 1)
            copy(stg[:, slot, :], pbig[:, bank(k, at, c), :]).then_inc(chunk_kept[c], 1)

        block = ctx.enter_context(nc.Block())

        @block.sync
        def _(sp):
            for s in chunk_stored:
                sp.sem_inc(s, 1)
            for s in chunk_kept:
                sp.sem_inc(s, 2)

            def lanes(a):
                return a.rearrange("(p c) -> p c", c=COLS)

            sp.dma_start(dst_c, lanes(dst)).then_inc(loaded_dst, 16)
            sp.dma_start(src_c, lanes(src)).then_inc(loaded_src, 16)
            sp.dma_start(wgt_c, lanes(weight)).then_inc(loaded_w, 16)
            sp.dma_start(typ_c, lanes(type_a)).then_inc(loaded_types, 16)
            sp.dma_start(typ_b, lanes(type_b)).then_inc(loaded_types, 16)
            sp.dma_start(basis_sb, basis.rearrange("b i o -> b (i o)")).then_inc(loaded_basis, 16)
            sp.dma_start(coeff_t[:, :], coeff.rearrange("r b -> b r"), allow_slow_non_contiguous=True).then_inc(loaded_basis, 16)
            sp.dma_start(bias_sb[:, :], bias.unsqueeze(0).to_broadcast([P, D])).then_inc(loaded_small, 16)
            sp.dma_start(beta_sb[:, :], beta.unsqueeze(0).to_broadcast([P, 2])).then_inc(loaded_small, 16)
            sp.wait_ge(relw_kept, 8)
            sp.dma_start(rel_w.rearrange("r i o -> r (i o)"), relw_sb).then_inc(relw_stored, 16)
            sp.wait_ge(padding_made, 1)
            sp.dma_start(bins.rearrange("(p n) f -> p (n f)", p=P), pd[:, 0:NI * 5]).then_inc(pads_stored, 16)

            def stage(n, s):
                sp.dma_start(slots[0:LANES, s, :, :], payd[:, bass.ds((n * 2 + s) * CH, CH), :]).then_inc(staged[s], 16)

            for part, end in enumerate(pl.ends):
                sp.wait_ge(pay_ready, part + 1)
                first = pl.ends[part - 1] if part else 1
                if part == 0:
                    for s in range(2):
                        stage(0, s)
                with sp.Fori(0, end - first) as t:
                    for s in range(2):
                        sp.wait_ge(scattered[s], (t + first) * (16 * CH))
                        stage(t + first, s)
            for s in range(2):
                sp.wait_ge(scattered[s], pl.stages * 16 * CH)
            sp.dma_start(pd[:, 0:NI * 5], bins.rearrange("(p n) f -> p (n f)", p=P)).then_inc(bins_loaded, 16)
            for k in (1, 2):
                sp.wait_ge(table_made, k + 1)
                sp.dma_start(tables[k].rearrange("(b p) f -> p b f", p=P), tab).then_inc(table_stored, 16)

            for k, table in enumerate((table_a, table_b)):
                view = table.rearrange("(b p r) f -> b p (r f)", p=P, b=NB)

                def store(at):
                    for c in range(PER[k]):
                        slot = at.slot * PER[k] + c
                        sp.wait_ge(chunk_kept[c], CB[k][c] + at.g + 3)
                        sp.dma_start(view[at.g, :, c * 512:(c + 1) * 512], stg[:, slot, :]).then_inc(chunk_stored[slot], 16)

                run_pass(sp, [(0, store)], count=NB, ring=2)
            sp.wait_ge(out_made, 1)
            sp.dma_start(out[0:FULL * P, :].rearrange("(b p) f -> p b f", p=P), x_sb[:, 0:FULL, :]).then_inc(out_stored, 16)
            if FULL < NB:
                sp.dma_start(out[FULL * P:, :], x_sb[0:pl.last, FULL, :]).then_inc(out_stored, 16)
            sp.wait_ge(out_stored, 16 * (1 + (FULL < NB)))

        @block.gpsimd
        def _(pool):
            pool.sem_inc(gathers_started, CREDIT)
            nc.gpsimd.iota(iota[:, :], pattern=[[1, WIDE]], base=0, channel_multiplier=0,
                           allow_small_or_imprecise_dtypes=True).then_inc(iota_made, 1)
            nc.gpsimd.iota(lane[:, :], pattern=[[0, 1]], base=0, channel_multiplier=1,
                           allow_small_or_imprecise_dtypes=True).then_inc(iota_made, 1)

            g = nc.gpsimd
            pool.wait_ge(relw_stored, 16)
            g.memset(pdi[:, :, 0], pl.nodes)
            g.memset(pdf[:, :, 1], -1.0)
            g.memset(pdf[:, :, 2], 0.0)
            g.memset(pdi[:, :, 3], pl.nodes * pl.rel_a)
            g.memset(pdi[:, :, 4], pl.nodes * pl.rel_b).then_inc(padding_made, 1)

            pool.wait_ge(pads_stored, 16)
            with pool.Fori(0, pl.stages) as t:
                for s in range(2):
                    pool.wait_ge(staged[s], (t + 1) * 16)
                    pool.sem_inc(scatters_started, 1)
                    for c in range(CH):
                        nc.gpsimd.indirect_dma_start(
                            bins, bass.IndirectOffsetOnAxis(ap=slots[0:LANES, s, c, 5:6], axis=0),
                            slots[0:LANES, s, c, 0:5], None).then_inc(scattered[s], 16)

            def gather(ps_):
                used = msg_made if ps_.softmax else summed
                width = ROW if ps_.softmax else D

                def fetch(at):
                    n = ps_.gather + at.g
                    u = at.g + (ps_.gather if ps_.softmax else ps_.every)
                    pool.wait_ge(idx_ready, done(n))
                    pool.wait_ge(used, done(u - RING))
                    pool.sem_inc(gathers_started, 1)
                    for j in range(ITEMS):
                        nc.gpsimd.indirect_dma_start(
                            rows[:, at.slot, j, 0:width], None, ps_.table,
                            bass.IndirectOffsetOnAxis(ap=idx[:, at.slot, j:j + 1], axis=0)).then_inc(gathered[at.slot], 16)
                run_pass(pool, [(0, fetch)])

            for k, ps_ in enumerate([p_edge] + p_agnn):
                pool.wait_ge(table_stored, 16 * (k + 1))
                gather(ps_)
            for k, ps_ in enumerate(p_plain):
                for slot in range(2 * PER[k]):
                    pool.wait_ge(chunk_stored[slot], 16 * (stores_before(k, slot) + blocks_of(slot // PER[k])) + 1)
                gather(ps_)

        @block.scalar
        def _(act):
            for s in (idx_ready, hot_t_made, pen_made, scored_b, keep_made, exp_made, ht_kept, hot_f_made):
                act.sem_inc(s, CREDIT)
            for k in range(8):
                act.wait_ge(relw_made, k + 1)
                nc.scalar.copy(relw_sb[:, k * 512:(k + 1) * 512], pbig[0:pl.rel_b, k % 4, :]).then_inc(relw_kept, 1)
            asked = [0]

            def root(col):
                asked[0] += 1
                act.wait_ge(dve_asks_act, asked[0])
                nc.scalar.activation(col, col, ACT.Sqrt).then_inc(act_answers, 1)

            def work(ps_):
                e = ps_.every

                def rows_wanted(at):
                    act.wait_ge(gathered[at.slot], ps_.gathers(at) * (16 * ITEMS))
                    nc.scalar.copy(idx[:, at.slot, :], pdi[:, bass.ds(at.g * ITEMS, ITEMS), ps_.column]).then_inc(idx_ready, 1)

                def turn_kept(at):
                    act.wait_ge(turned, done(e + at.g))
                    nc.scalar.copy(hot_t[:, at.slot, :, :].rearrange("p j e -> p (j e)"), p_t[:, at.two, 0:ITEMS * P]).then_inc(hot_t_made, 1)

                def penalty(at):
                    nc.scalar.activation(pen_t[:, at.three, :], p_t[:, at.two, 0:ITEMS * P], ACT.Identity,
                                         bias=neg_big[:, 0:1], scale=BIG).then_inc(pen_made, 1)

                def exponentials(at):
                    act.wait_ge(shift_made, done(e + at.g))
                    act.wait_ge(msg_made, done(ps_.gather + at.g - 2))
                    if ps_.kind == EDGE:
                        nc.scalar.activation(expd[:, at.two, :, :], shifted[:, at.two, :, :], ACT.Exp).then_inc(exp_made, 1)
                    else:
                        nc.scalar.activation(expd[:, at.two, 0, :], shifted[:, at.two, 0, :], ACT.Exp).then_inc(exp_made, 1)

                def factors(at):
                    act.wait_ge(risen, done(e + at.g))
                    last = nc.scalar.activation(keep[:, at.slot, 0:1], rise[:, at.three:at.three + 1], ACT.Exp, scale=-1.0)
                    if ps_.kind == EDGE:
                        last = nc.scalar.activation(keep[:, at.slot, 1:2], rise[:, at.three:at.three + 1], ACT.Exp, scale=-0.5)
                    last.then_inc(keep_made, 1)

                def scores_rounded(at):
                    act.wait_ge(spread, done(e + at.g - 2))
                    if ps_.kind == AGNN:
                        act.wait_ge(scored, done(ps_.own + at.g))
                        nc.scalar.copy(score_b[:, at.two, :], score[:, at.three, :]).then_inc(scored_b, 1)
                    else:
                        nc.scalar.copy(score_b[:, at.two, :], ps_.weight[:, bass.ds(at.g * ITEMS, ITEMS)]).then_inc(scored_b, 1)

                def hot_widened(at):
                    act.wait_ge(summed, done(e + at.g - 2))
                    nc.scalar.copy(hot_f[:, at.two, :, :], hot[:, at.slot, :, :]).then_inc(hot_f_made, 1)

                steps = []
                if ps_.softmax:
                    steps += [(1, turn_kept), (-1, exponentials), (1, penalty), (-1, hot_widened),
                              (0, factors), (1, scores_rounded)]
                steps += [(RING - 1, rows_wanted)]
                run_pass(act, steps)

            def build(k):
                def turned_kept(at):
                    act.wait_ge(blk_turned, done(k * NB + at.g))
                    act.wait_ge(chunk_made[PER[k] - 1], done(CB[k][-1] + at.g - 2))
                    nc.scalar.copy(ht[:, at.slot, :], p_turn[:, at.slot, :]).then_inc(ht_kept, 1)

                def pieces(at):
                    for c in range(PER[k]):
                        if c not in ON_DVE[k]:
                            copy_piece(act, nc.scalar.copy, k, at, c)

                run_pass(act, [(1, turned_kept), (0, pieces)], count=NB, ring=2)

            act.wait_ge(consts_made, 1)
            act.wait_ge(less_guard, 1)
            nc.scalar.activation(exp_c, exp_c, ACT.Exp).then_inc(exps_made, 1)
            act.wait_ge(x_cleared, 1)
            act.dma_start(x_sb[:, 0:FULL, :], x[0:FULL * P, :].rearrange("(b p) f -> p b f", p=P)).then_inc(x_loaded, 16)
            if FULL < NB:
                act.dma_start(x_sb[0:pl.last, FULL, :], x[FULL * P:, :]).then_inc(x_loaded, 16)
            act.wait_ge(relw_stored, 16)
            at = 0
            for given, rels in ((w_a, pl.rel_a), (rel_w, pl.rel_b), (w_self.unsqueeze(0), 1)):
                for half in range(2):
                    act.dma_start(w_f32[half * D:(half + 1) * D, at * D:(at + rels) * D].rearrange("i (r o) -> i r o", o=D),
                                  given.rearrange("r i o -> i r o")).then_inc(weights_loaded, 16)
                at += rels
            root(col_a[:, :])
            asked[0] += 1
            act.wait_ge(dve_asks_act, asked[0])
            nc.scalar.activation(col_b[:, :], col_b[:, :], ACT.Ln).then_inc(act_answers, 1)
            act.wait_ge(table_made, 1)
            act.dma_start(tables[0].rearrange("(b p) f -> p b f", p=P), tab).then_inc(table_stored, 16)
            act.wait_ge(bins_loaded, 16)
            work(p_edge)
            root(col_a[:, :])
            root(col_a[:, :])
            root(col_a[:, :])
            work(p_agnn[0])
            root(col_a[:, :])
            work(p_agnn[1])

            root(col_a[:, :])
            build(0)
            work(p_plain[0])
            root(col_a[:, :])
            build(1)
            work(p_plain[1])

        @block.vector
        def _(dve):
            for s in (hot_made, hot_f_direct, multiplied, dotted, scored, group_max, max_made, risen, max_kept,
                      shift_made, unsourced, msg_made, added, blk_high, blk_less, blk_mid, blk_split, self_added):
                dve.sem_inc(s, CREDIT)
            steps = [0]

            def link(ins):
                steps[0] += 1
                ins.then_inc(dve_step, 1)
                dve.wait_ge(dve_step, steps[0])

            def linked(t, per, k):
                return steps[0] + t * per + k

            asked = [0]

            def ask(ins):
                asked[0] += 1
                ins.then_inc(dve_asks_act, 1)
                dve.wait_ge(act_answers, asked[0])

            v = nc.vector
            dve.wait_ge(iota_made, 2)
            v.tensor_scalar(ident[:, :], iota[:, 0:P], lane[:, 0:1], None, ALU.is_equal)
            v.tensor_scalar(ident_b[:, :], iota[:, 0:P], lane[:, 0:1], None, ALU.is_equal)
            v.tensor_scalar(before[:, :], iota[:, 0:P], lane[:, 0:1], None, ALU.is_gt)
            v.tensor_copy(iota_b[:, :], iota[:, 0:P])
            v.memset(ones[:, :], 1.0)
            v.memset(bin_zero[:, :], 0.0)
            link(v.memset(neg_big[:, :], -BIG))
            v.memset(lane_bin[:, :], 0.0).then_inc(consts_made, 1)

            dve.wait_ge(loaded_dst, 16)
            link(v.tensor_scalar(tmp_i, dst_c, 7, None, ALU.arith_shift_right))
            link(v.tensor_copy(bin_c, tmp_i))
            link(v.tensor_scalar(tmp_i, dst_c, 127, None, ALU.bitwise_and))
            link(v.tensor_copy(paydf[:, :, 1], tmp_i))
            with dve.Fori(0, NB) as b:
                v.tensor_scalar(hot_c, bin_c, iota[0:LANES, bass.ds(b, 1)], None, ALU.is_equal, ALU.add,
                                accum_out=lane_bin[0:LANES, bass.ds(b, 1)]).then_inc(dve_step, 1)
                dve.wait_ge(dve_step, linked(b, 1, 1))
            steps[0] += NB
            v.engine_nop().then_inc(counted, 1)
            dve.wait_ge(offsets_made, 1)
            link(v.tensor_scalar(bin_groups_i[:, :], p_cnt[:, 64:64 + NB], float(P - 1), None, ALU.add))
            link(v.tensor_scalar(bin_groups_i[:, :], bin_groups_i[:, :], 7, None, ALU.arith_shift_right))
            link(v.tensor_scalar(bin_groups_i[:, :], bin_groups_i[:, :], float(ITEMS - 1), float(pl.ratio), ALU.add, ALU.mult))
            link(v.tensor_scalar(bin_groups_i[:, :], bin_groups_i[:, :], pl.shift, None, ALU.arith_shift_right))
            link(v.tensor_copy(bin_groups[:, :], bin_groups_i[:, :]))
            link(v.tensor_tensor_scan(bin_first[:, :], bin_groups[:, :], bin_zero[:, :], 0.0, ALU.add, ALU.add))
            link(v.tensor_tensor(bin_first[:, :], bin_first[:, :], bin_groups[:, :], ALU.subtract))
            v.engine_nop().then_inc(first_made, 1)
            link(v.tensor_scalar(bin_from[:, :], bin_first[:, :], float(ITEMS * P), -1.0, ALU.mult, ALU.add))
            link(v.tensor_tensor(bin_from[0:LANES, :], bin_from[0:LANES, :], p_cnt[0:LANES, 0:NB], ALU.add))
            dve.wait_ge(first_col_made, 1)
            link(v.tensor_copy(first_col[:, :], p_col[0:NB, 0:1]))
            v.tensor_scalar(reached[:, :], iota[0:NB, 0:NG], first_col[:, 0:1], None, ALU.is_ge).then_inc(reached_made, 1)
            dve.wait_ge(block_made, 1)
            v.tensor_scalar(group_block[:, :], pbig[0:1, :, :].rearrange("p b c -> p (b c)")[:, 0:NG], -1.0, None, ALU.add).then_inc(blocks_ready, 1)
            link(v.memset(pos_c, 0.0))
            dve.wait_ge(loaded_src, 16)
            dve.wait_ge(loaded_w, 16)
            dve.wait_ge(loaded_types, 32)
            for start, end in zip([0] + pl.ends, pl.ends):
                cut = slice(start * 2 * CH, end * 2 * CH)
                with dve.Fori(0, NB) as b:
                    run_from = bin_from[0:LANES, bass.ds(b, 1)]
                    v.tensor_scalar(hot_c[:, cut], bin_c[:, cut], iota[0:LANES, bass.ds(b, 1)], None, ALU.is_equal).then_inc(dve_step, 1)
                    dve.wait_ge(dve_step, linked(b, 5, 1))
                    v.tensor_tensor_scan(run_c[:, cut], hot_c[:, cut], hot_c[:, cut], run_from, ALU.add, ALU.bypass).then_inc(dve_step, 1)
                    dve.wait_ge(dve_step, linked(b, 5, 2))
                    v.tensor_tensor(tmp_c[:, cut], hot_c[:, cut], run_c[:, cut], ALU.mult).then_inc(dve_step, 1)
                    v.tensor_scalar(run_from, run_c[:, cut.stop - 1:cut.stop], 1.0, None, ALU.mult).then_inc(dve_step, 1)
                    dve.wait_ge(dve_step, linked(b, 5, 4))
                    v.tensor_tensor(pos_c[:, cut], pos_c[:, cut], tmp_c[:, cut], ALU.add).then_inc(dve_step, 1)
                    dve.wait_ge(dve_step, linked(b, 5, 5))
                steps[0] += 5 * NB
                v.tensor_copy(payd[:, cut, 0], src_c[:, cut])
                v.tensor_copy(paydf[:, cut, 2], wgt_c[:, cut])
                for field, typ, rels in ((3, typ_c, pl.rel_a), (4, typ_b, pl.rel_b)):
                    v.scalar_tensor_tensor(out=payd[:, cut, field], in0=src_c[:, cut], scalar=float(rels), in1=typ[:, cut],
                                           op0=ALU.mult, op1=ALU.add)
                link(v.tensor_copy(tmp_i[:, cut], pos_c[:, cut]))
                link(v.tensor_scalar(run_i[:, cut], tmp_i[:, cut], 127, None, ALU.bitwise_and))
                link(v.tensor_scalar(tmp_i[:, cut], tmp_i[:, cut], 7, None, ALU.arith_shift_right))
                link(v.scalar_tensor_tensor(out=payd[:, cut, 5], in0=run_i[:, cut], scalar=float(NI), in1=tmp_i[:, cut],
                                            op0=ALU.mult, op1=ALU.add))
                v.engine_nop().then_inc(pay_ready, 1)

            link(v.tensor_scalar(tmp_i, src_c, 7, None, ALU.arith_shift_right))
            link(v.tensor_copy(high_c, tmp_i))
            link(v.tensor_scalar(tmp_i, src_c, 127, None, ALU.bitwise_and))
            link(v.tensor_copy(low_c, tmp_i))
            link(v.tensor_scalar(tmp_c, wgt_c, -1.0, None, ALU.mult))
            v.reduce_max(extremes[0:LANES, 0:1], wgt_c, AX)
            v.reduce_max(extremes[0:LANES, 1:2], tmp_c, AX).then_inc(extremes_made, 1)
            dve.wait_ge(extremes_turned, 1)
            link(v.reduce_max(spread_of[:, 0:2], p_max[0:1, 0:2 * P].rearrange("p (k l) -> p k l", k=2)[:, :, 0:LANES], AX))
            link(v.tensor_tensor(spread_of[:, 2:3], spread_of[:, 0:1], spread_of[:, 1:2], ALU.add))
            link(v.tensor_scalar(wide[:, :], spread_of[:, 2:3], RANGE, None, ALU.is_gt))
            v.engine_nop().then_inc(wide_made, 1)
            dve.wait_ge(guard_spread, 1)
            link(v.tensor_copy(guard[:, :], p_max[:, 2 * P:2 * P + 1]))
            v.tensor_copy(run_max[:, :], guard[:, 0:1].to_broadcast([P, NB]))
            link(v.tensor_scalar(exp_c, wgt_c, guard[0:LANES, 0:1], None, ALU.subtract))

            is_wide = nc.values_load_multi_w_load_instructions(
                wide[0:1, 0:1], engines=[dve.engine], min_val=0, max_val=1,
                skip_runtime_bounds_check_because="the result of a comparison")[1][0]
            with dve.If(is_wide == 1):
                v.tensor_copy(src_f, src_c)
                v.tensor_copy(exp_c, wgt_c)
                v.memset(node_no[:, :], 0.0).then_inc(wide_set, 1)
                dve.wait_ge(wide_set, 1)
                with dve.Fori(0, NB) as b:
                    with dve.Fori(0, P) as n:
                        i = b * P + n
                        v.tensor_scalar(tmp_c, src_f, node_no[0:LANES, 0:1], -BIG, ALU.not_equal, ALU.mult).then_inc(masked, 1)
                        dve.wait_ge(masked, i + 1)
                        v.tensor_tensor(tmp_c, tmp_c, wgt_c, ALU.add).then_inc(joined, 1)
                        v.tensor_scalar(node_no[:, 0:1], node_no[:, 0:1], 1.0, None, ALU.add).then_inc(numbered, 1)
                        dve.wait_ge(joined, i + 1)
                        dve.wait_ge(numbered, i + 1)
                        v.reduce_max(cand[0:LANES, bass.ds(n, 1)], tmp_c, AX).then_inc(reduced, 1)
                        dve.wait_ge(reduced, i + 1)
                    v.engine_nop().then_inc(cand_made, 1)
                    dve.wait_ge(cand_turned, b + 1)
                    v.reduce_max(block_max[:, :], p_max[:, 0:LANES], AX).then_inc(block_max_made, 1)
                    dve.wait_ge(block_max_made, b + 1)
                    dve.wait_ge(node_max_spread, b + 1)
                    v.tensor_copy(node_max[0:LANES, :], p_max[0:LANES, 0:P]).then_inc(node_max_kept, 1)
                    dve.wait_ge(node_max_kept, b + 1)
                    v.tensor_scalar(run_max[:, bass.ds(b, 1)], block_max[:, :], 1.0, None, ALU.mult)
                    with dve.Fori(0, P) as n:
                        i = b * P + n
                        v.tensor_scalar(tmp_c, src_f, node_no[0:LANES, 1:2], node_max[0:LANES, bass.ds(n, 1)],
                                        ALU.is_equal, ALU.mult).then_inc(taken, 1)
                        dve.wait_ge(taken, i + 1)
                        v.tensor_scalar(node_no[:, 1:2], node_no[:, 1:2], 1.0, None, ALU.add).then_inc(numbered_2, 1)
                        v.tensor_tensor(exp_c, exp_c, tmp_c, ALU.subtract).then_inc(lessened, 1)
                        dve.wait_ge(numbered_2, i + 1)
                        dve.wait_ge(lessened, i + 1)
                v.engine_nop().then_inc(wide_set, 1)
            v.engine_nop().then_inc(less_guard, 1)
            dve.wait_ge(exps_made, 1)

            def piece(at):
                cols = bass.ds(at.g * PC, PC)
                dve.wait_ge(piece_used, at.g + 1)
                v.tensor_tensor(high_exp[:, at.slot, :, :], iota[0:LANES, 0:NB].unsqueeze(1).to_broadcast([LANES, PC, NB]),
                                high_c[:, cols].unsqueeze(2).to_broadcast([LANES, PC, NB]), ALU.is_equal).then_inc(high_made, 1)
                v.tensor_tensor(low_hot[:, at.slot, :, :], iota[0:LANES, 0:P].unsqueeze(1).to_broadcast([LANES, PC, P]),
                                low_c[:, cols].unsqueeze(2).to_broadcast([LANES, PC, P]), ALU.is_equal)
                dve.wait_ge(high_made, at.g + 1)
                v.tensor_tensor(high_exp[:, at.slot, :, :], high_exp[:, at.slot, :, :],
                                exp_c[:, cols].unsqueeze(2).to_broadcast([LANES, PC, NB]), ALU.mult).then_inc(piece_made, 1)

            run_pass(dve, [(0, piece)], count=COLS // PC, ring=2)
            dve.wait_ge(out_summed, 1)
            link(v.tensor_copy(out_sum[:, :], p_sum[:, 0:NB]))
            v.memset(x_sb[:, :, :], 0.0).then_inc(x_cleared, 1)

            def bc(col, n=D):
                return col.unsqueeze(2).to_broadcast([P, NB, n])

            def layer_norm():
                link(v.reduce_sum(col_a[:, :], x_sb[:, :, :], AX))
                link(v.tensor_scalar(col_a[:, :], col_a[:, :], 1.0 / D, None, ALU.mult))
                link(v.tensor_tensor(h_sb[:, :, :], x_sb[:, :, :], bc(col_a[:, :]), ALU.subtract))
                link(v.tensor_tensor(sq[:, :, :], h_sb[:, :, :], h_sb[:, :, :], ALU.mult))
                link(v.reduce_sum(col_a[:, :], sq[:, :, :], AX))
                ask(v.tensor_scalar(col_a[:, :], col_a[:, :], 1.0 / D, LN_EPS, ALU.mult, ALU.add))
                link(v.reciprocal(col_a[:, :], col_a[:, :]))
                link(v.scalar_tensor_tensor(out=h_sb[:, :, :], in0=h_sb[:, :, :], scalar=0.0, in1=bc(col_a[:, :]),
                                            op0=ALU.max, op1=ALU.mult))

            def agnn_table(k):
                link(v.tensor_tensor(sq[:, :, :], h_sb[:, :, :], h_sb[:, :, :], ALU.mult))
                ask(v.reduce_sum(col_a[:, :], sq[:, :, :], AX))
                link(v.tensor_scalar(col_a[:, :], col_a[:, :], NORM_EPS, None, ALU.max))
                link(v.reciprocal(col_a[:, :], col_a[:, :]))
                v.tensor_scalar(tab[:, :, D], col_a[:, :], beta_sb[:, k:k + 1], None, ALU.mult)
                v.tensor_copy(tab[:, :, 0:D], h_sb[:, :, :]).then_inc(table_made, 1)
                link(v.tensor_tensor(unit[:, :, :], h_sb[:, :, :], bc(col_a[:, :]), ALU.mult))
                for part in range(3):
                    link(v.tensor_copy(unit3[:, part, :, :], unit[:, :, :]))
                    if part < 2:
                        link(v.tensor_tensor(unit[:, :, :], unit[:, :, :], unit3[:, part, :, :], ALU.subtract))
                v.engine_nop().then_inc(units_made, 1)

            def clear_sums():
                v.memset(run_max[:, :], -BIG)
                link(v.memset(acc[:, :, :], 0.0))

            def work(ps_):
                e = ps_.every

                def items(a, at):
                    return a[:, bass.ds(at.g * ITEMS, ITEMS)]

                def one_hots(at):
                    nodes = items(ps_.local, at).unsqueeze(2).to_broadcast([P, ITEMS, P])
                    if ps_.softmax:
                        v.tensor_tensor(hot[:, at.slot, :, :], iota_b[:, :].unsqueeze(1).to_broadcast([P, ITEMS, P]),
                                        nodes, ALU.is_equal).then_inc(hot_made, 1)
                    else:
                        dve.wait_ge(summed, done(e + at.g - 2))
                        v.tensor_tensor(hot_f[:, at.two, :, :], iota[:, 0:P].unsqueeze(1).to_broadcast([P, ITEMS, P]),
                                        nodes, ALU.is_equal).then_inc(hot_f_direct, 1)

                def multiply(at):
                    dve.wait_ge(gathered[at.slot], (ps_.gathers(at) + 1) * (16 * ITEMS))
                    dve.wait_ge(dst_rows, done(ps_.own + at.g))
                    v.tensor_tensor(prod[:, at.two, :, :], rows[:, at.slot, :, 0:D], p_row[:, at.two, :, :],
                                    ALU.mult).then_inc(multiplied, 1)

                def dot_products(at):
                    dve.wait_ge(multiplied, done(ps_.own + at.g))
                    v.reduce_sum(dot[:, at.two, :], prod[:, at.two, :, :], AX).then_inc(dotted, 1)

                def scores(at):
                    dve.wait_ge(dotted, done(ps_.own + at.g))
                    v.tensor_tensor(score[:, at.three, :], dot[:, at.two, :], rows[:, at.slot, :, D], ALU.mult).then_inc(scored, 1)

                def group_maxima(at):
                    dve.wait_ge(spread, done(e + at.g))
                    v.reduce_max(gmax[:, at.two:at.two + 1], p_v[:, at.two, 0:ITEMS * P], AX).then_inc(group_max, 1)

                def new_maxima(at):
                    kept, group = run_max[:, bass.ds(at.block, 1)], gmax[:, at.two:at.two + 1]
                    dve.wait_ge(group_max, done(e + at.g))
                    v.tensor_tensor(new_max[:, at.two:at.two + 1], kept, group, ALU.max).then_inc(max_made, 1)
                    v.scalar_tensor_tensor(out=rise[:, at.three:at.three + 1], in0=kept, scalar=group, in1=kept,
                                           op0=ALU.max, op1=ALU.subtract).then_inc(risen, 1)

                def keep_maxima(at):
                    kept = run_max[:, bass.ds(at.block, 1)]
                    dve.wait_ge(risen, done(e + at.g))
                    v.tensor_tensor(kept, kept, gmax[:, at.two:at.two + 1], ALU.max).then_inc(max_kept, 1)

                def less_maxima(at):
                    two = at.two
                    if ps_.kind == EDGE:
                        dve.wait_ge(gathered[at.slot], (ps_.gathers(at) + 1) * (16 * ITEMS))
                        v.tensor_tensor(less_src[:, two, :], items(ps_.weight, at), rows[:, at.slot, :, D], ALU.subtract).then_inc(unsourced, 1)
                    dve.wait_ge(edge_max, done(e + at.g))
                    if ps_.kind == AGNN:
                        v.tensor_tensor(shifted[:, two, 0, :], score[:, at.three, :], p_max[:, 0:ITEMS], ALU.subtract).then_inc(shift_made, 1)
                    else:
                        v.tensor_tensor(shifted[:, two, 0, :], items(ps_.weight, at), p_max[:, 0:ITEMS], ALU.subtract)
                        dve.wait_ge(unsourced, done(at.g))
                        v.scalar_tensor_tensor(out=shifted[:, two, 1, :], in0=p_max[:, 0:ITEMS], scalar=-0.5,
                                               in1=less_src[:, two, :], op0=ALU.mult, op1=ALU.add).then_inc(shift_made, 1)

                def messages(at):
                    dve.wait_ge(exp_made, done(e + at.g))
                    v.tensor_copy(msg[:, at.two, :, D], expd[:, at.two, 0, :])
                    v.tensor_tensor(msg[:, at.two, :, 0:D], rows[:, at.slot, :, 0:D],
                                    expd[:, at.two, int(ps_.kind == EDGE), :].unsqueeze(2).to_broadcast([P, ITEMS, D]),
                                    ALU.mult).then_inc(msg_made, 1)

                def sums(at):
                    b = at.block
                    dve.wait_ge(summed, done(e + at.g))
                    keep_1, keep_half = keep[:, at.slot, 0:1], keep[:, at.slot, 1:2]
                    if ps_.kind == EDGE:
                        v.scalar_tensor_tensor(out=acc[:, b, 0:D], in0=acc[:, b, 0:D], scalar=keep_half,
                                               in1=p_sum[:, 0:D], op0=ALU.mult, op1=ALU.add)
                        v.scalar_tensor_tensor(out=acc[:, b, D:ROW], in0=acc[:, b, D:ROW], scalar=keep_1,
                                               in1=p_sum[:, D:ROW], op0=ALU.mult, op1=ALU.add).then_inc(added, 1)
                    elif ps_.kind == AGNN:
                        v.scalar_tensor_tensor(out=acc[:, b, :], in0=acc[:, b, :], scalar=keep_1,
                                               in1=p_sum[:, 0:ROW], op0=ALU.mult, op1=ALU.add).then_inc(added, 1)
                    else:
                        v.tensor_tensor(acc[:, b, :], acc[:, b, :], p_sum[:, 0:ROW], ALU.add).then_inc(added, 1)

                if ps_.kind == PLAIN:
                    run_pass(dve, [(1, one_hots), (-1, sums)], ps_.block, (-1, -1))
                else:
                    steps = [(-3, sums), (-1, less_maxima), (3, one_hots), (0, group_maxima)]
                    steps += [(1, multiply)] * (ps_.kind == AGNN) + [(0, new_maxima)]
                    steps += [(1, dot_products)] * (ps_.kind == AGNN) + [(0, keep_maxima)]
                    steps += [(1, scores)] * (ps_.kind == AGNN) + [(-1, messages)]
                    run_pass(dve, steps, ps_.block, (-3, 0))
                dve.wait_ge(added, done(e + NG - 1))

            def build(k):
                def split(at):
                    n, two = k * NB + at.g, at.slot
                    four = h_parts[:, two, :].rearrange("p (q f) -> p q f", f=D)
                    dve.wait_ge(blk_turned, done(n - 2))
                    v.tensor_scalar(four[:, 0:3:2, :], h_sb[:, at.g, :].unsqueeze(1).to_broadcast([P, 2, D]), 1.0, None,
                                    ALU.mult).then_inc(blk_high, 1)
                    dve.wait_ge(blk_high, done(n))
                    v.tensor_tensor(h_rest[:, two, :], h_sb[:, at.g, :], four[:, 0, :], ALU.subtract).then_inc(blk_less, 1)
                    dve.wait_ge(blk_less, done(n))
                    v.tensor_copy(four[:, 1, :], h_rest[:, two, :]).then_inc(blk_mid, 1)
                    dve.wait_ge(blk_mid, done(n))
                    v.tensor_tensor(four[:, 3, :], h_rest[:, two, :], four[:, 1, :], ALU.subtract).then_inc(blk_split, 1)

                def pieces(at):
                    for c in ON_DVE[k]:
                        copy_piece(dve, v.tensor_copy, k, at, c)

                def self_sums(at):
                    dve.wait_ge(self_made, done(at.g))
                    v.tensor_tensor(x_sb[:, at.g, :], x_sb[:, at.g, :], p_sum[:, 0:D], ALU.add).then_inc(self_added, 1)

                run_pass(dve, [(2, split), (0, pieces)] + [(0, self_sums)] * k, count=NB, ring=2)

            dve.wait_ge(weights_loaded, 96)
            link(v.tensor_copy(w_parts[:, 0, :], w_f32))
            link(v.tensor_tensor(w_f32, w_f32, w_parts[:, 0, :], ALU.subtract))
            link(v.tensor_copy(w_parts[:, 1, :], w_f32))
            link(v.tensor_tensor(w_parts[0:D, 2, :], w_f32[0:D, :], w_parts[0:D, 1, :], ALU.subtract))
            link(v.tensor_copy(w_parts[D:P, 2, :], w_parts[D:P, 0, :]))
            v.engine_nop().then_inc(weights_split, 1)
            dve.wait_ge(x_loaded, 16 * (1 + (FULL < NB)))
            layer_norm()
            link(v.tensor_scalar(col_b[:, :], out_sum[:, :], 2.0 ** -60, None, ALU.max))
            link(v.tensor_scalar(col_c[:, :], out_sum[:, :], 2.0 ** -59, 0.5, ALU.is_gt, ALU.mult))
            ask(v.engine_nop())
            link(v.tensor_tensor(col_b[:, :], col_b[:, :], run_max[:, :], ALU.add))
            link(v.tensor_tensor(tab[:, :, D], col_b[:, :], col_c[:, :], ALU.mult))
            v.tensor_copy(tab[:, :, 0:D], h_sb[:, :, :]).then_inc(table_made, 1)
            dve.wait_ge(bins_loaded, 16)
            clear_sums()
            work(p_edge)
            link(v.tensor_scalar(col_a[:, :], acc[:, :, D], 1e-30, None, ALU.max))
            ask(v.engine_nop())
            link(v.reciprocal(col_a[:, :], col_a[:, :]))
            link(v.tensor_tensor(acc[:, :, 0:D], acc[:, :, 0:D], bc(col_a[:, :]), ALU.mult))
            link(v.tensor_tensor(x_sb[:, :, :], x_sb[:, :, :], acc[:, :, 0:D], ALU.add))

            layer_norm()
            dve.wait_ge(loaded_small, 32)
            for k in range(2):
                agnn_table(k)
                clear_sums()
                work(p_agnn[k])
                link(v.tensor_scalar(col_a[:, :], acc[:, :, D], 1e-30, None, ALU.max))
                link(v.reciprocal(col_a[:, :], col_a[:, :]))
                link(v.scalar_tensor_tensor(out=h_sb[:, :, :], in0=acc[:, :, 0:D], scalar=0.0, in1=bc(col_a[:, :]),
                                            op0=ALU.max, op1=ALU.mult))
            link(v.tensor_tensor(x_sb[:, :, :], x_sb[:, :, :], h_sb[:, :, :], ALU.add))

            layer_norm()
            build(0)
            v.memset(rows[:, :, :, D], 1.0)
            clear_sums()
            work(p_plain[0])
            link(v.tensor_tensor(x_sb[:, :, :], x_sb[:, :, :], acc[:, :, 0:D], ALU.add))

            layer_norm()
            link(v.tensor_tensor(x_sb[:, :, :], x_sb[:, :, :], bias_sb[:, :].unsqueeze(1).to_broadcast([P, NB, D]), ALU.add))
            build(1)
            clear_sums()
            work(p_plain[1])
            link(v.tensor_scalar(col_a[:, :], acc[:, :, D], 1.0, None, ALU.max))
            link(v.reciprocal(col_a[:, :], col_a[:, :]))
            link(v.tensor_tensor(acc[:, :, 0:D], acc[:, :, 0:D], bc(col_a[:, :]), ALU.mult))
            v.tensor_tensor(x_sb[:, :, :], x_sb[:, :, :], acc[:, :, 0:D], ALU.add).then_inc(out_made, 1)

        @block.tensor
        def _(pe):
            for s in (turned, dst_rows, spread, edge_max, summed, blk_turned, self_made, *chunk_made):
                pe.sem_inc(s, CREDIT)
            mm = nc.tensor.matmul
            pe.wait_ge(loaded_basis, 32)
            for k in range(8):
                if k >= 4:
                    pe.wait_ge(relw_kept, k - 3)
                mm(pbig[0:pl.rel_b, k % 4, :], coeff_t[:, :], basis_sb[:, k * 512:(k + 1) * 512],
                   start=True, stop=True).then_inc(relw_made, 1)
            pe.wait_ge(consts_made, 1)
            pe.wait_ge(relw_kept, 8)
            pe.wait_ge(counted, 1)
            mm(p_cnt[0:LANES, 0:NB], before[0:LANES, 0:LANES], lane_bin[0:LANES, :], start=True, stop=True)
            mm(p_cnt[:, 64:64 + NB], ones[0:LANES, :], lane_bin[0:LANES, :], start=True, stop=True).then_inc(offsets_made, 1)
            pe.wait_ge(first_made, 1)
            mm(p_col[0:NB, 0:1], bin_first[0:1, :], ones[0:1, 0:1], start=True, stop=True).then_inc(first_col_made, 1)
            pe.wait_ge(reached_made, 1)
            for c in range(0, NG, 512):
                n = min(512, NG - c)
                last = mm(pbig[0:1, c // 512, 0:n], ones[0:NB, 0:1], reached[:, c:c + n], start=True, stop=True)
            last.then_inc(block_made, 1)
            pe.wait_ge(extremes_made, 1)
            for k in range(2):
                last = mm(p_max[0:1, k * P:k * P + LANES], extremes[0:LANES, k:k + 1], ident[0:LANES, 0:LANES],
                          start=True, stop=True)
            last.then_inc(extremes_turned, 1)
            pe.wait_ge(wide_made, 1)
            mm(p_max[:, 2 * P:2 * P + 1], ones[0:1, :], spread_of[0:1, 0:1], start=True, stop=True).then_inc(guard_spread, 1)
            is_wide = nc.values_load_multi_w_load_instructions(
                wide[0:1, 0:1], engines=[pe.engine], min_val=0, max_val=1,
                skip_runtime_bounds_check_because="the result of a comparison")[1][0]
            with pe.If(is_wide == 1):
                with pe.Fori(0, NB) as b:
                    pe.wait_ge(cand_made, b + 1)
                    mm(p_max[:, 0:LANES], cand[0:LANES, :], ident[0:LANES, 0:LANES], start=True, stop=True).then_inc(cand_turned, 1)
                    pe.wait_ge(block_max_made, b + 1)
                    mm(p_max[0:LANES, 0:P], block_max[:, 0:1].to_broadcast([P, LANES]), ident[:, :],
                       start=True, stop=True).then_inc(node_max_spread, 1)
            pe.sem_inc(piece_used, 2)
            mm(p_sum[:, 0:NB], ones[:, :], bin_zero[:, :], start=True, stop=False)

            def sum_piece(at):
                pe.wait_ge(piece_made, at.g + 1)
                for c in range(PC):
                    last = mm(p_sum[:, 0:NB], low_hot[:, at.slot, c, :], high_exp[:, at.slot, c, :], start=False, stop=False)
                last.then_inc(piece_used, 1)

            run_pass(pe, [(0, sum_piece)], count=COLS // PC, ring=2)
            mm(p_sum[:, 0:NB], ones[:, :], bin_zero[:, :], start=False, stop=True).then_inc(out_summed, 1)

            def work(ps_):
                e = ps_.every

                def turned_hots(at):
                    pe.wait_ge(hot_made, done(e + at.g))
                    for j in range(ITEMS):
                        last = nc.tensor.transpose(p_t[:, at.two, j * P:(j + 1) * P], hot[:, at.slot, j, :], ident_b[:, :])
                    last.then_inc(turned, 1)

                def rows_of_destinations(at):
                    b = at.block
                    pe.wait_ge(hot_t_made, done(e + at.g))
                    for j in range(ITEMS):
                        for part in range(3):
                            last = mm(p_row[:, at.two, j, :], hot_t[:, at.slot, j, :], unit3[:, part, b, :],
                                      start=part == 0, stop=part == 2)
                    last.then_inc(dst_rows, 1)

                def spread_scores(at):
                    pe.wait_ge(scored_b, done(e + at.g))
                    mm(p_v[:, at.two, 0:ITEMS * P], ident_b[:, :], pen_t[:, at.three, :], start=True, stop=False)
                    for j in range(ITEMS):
                        last = mm(p_v[:, at.two, j * P:(j + 1) * P], score_b[:, at.two, j:j + 1].to_broadcast([P, P]),
                                  ident_b[:, :], start=False, stop=j == ITEMS - 1)
                    last.then_inc(spread, 1)

                def maxima_of_edges(at):
                    pe.wait_ge(max_made, done(e + at.g))
                    for j in range(ITEMS):
                        last = mm(p_max[:, j:j + 1], hot_t[:, at.slot, j, :], new_max[:, at.two:at.two + 1],
                                  start=True, stop=True)
                    last.then_inc(edge_max, 1)

                def sums_per_node(at):
                    pe.wait_ge(added, done(e + at.g - 1))
                    if ps_.softmax:
                        pe.wait_ge(hot_f_made, done(e + at.g))
                    else:
                        pe.wait_ge(hot_f_direct, done(ps_.own + at.g))
                    if ps_.softmax:
                        pe.wait_ge(msg_made, done(ps_.gather + at.g))
                    else:
                        pe.wait_ge(gathered[at.slot], (ps_.gathers(at) + 1) * (16 * ITEMS))
                    for j in range(ITEMS):
                        if ps_.softmax:
                            given = msg[:, at.two, j, :]
                        else:
                            given = rows[:, at.slot, j, :]
                        last = mm(p_sum[:, 0:given.shape[1]], hot_f[:, at.two, j, :], given,
                                  start=j == 0, stop=j == ITEMS - 1)
                    last.then_inc(summed, 1)

                if ps_.kind == PLAIN:
                    run_pass(pe, [(0, sums_per_node)])
                elif ps_.kind == AGNN:
                    run_pass(pe, [(-1, maxima_of_edges), (0, spread_scores), (1, rows_of_destinations),
                                  (-2, sums_per_node), (2, turned_hots)], ps_.block, (1, 1))
                else:
                    run_pass(pe, [(-1, maxima_of_edges), (0, spread_scores), (-2, sums_per_node), (2, turned_hots)])

            def build(k):
                first_col_of = (0, pl.rel_a * D)[k]

                def turn_blocks(at):
                    pe.wait_ge(blk_split, done(k * NB + at.g))
                    for q in range(2):
                        last = nc.tensor.transpose(p_turn[:, at.slot, q * P:(q + 1) * P], h_parts[:, at.slot, q * P:(q + 1) * P], ident_b[:, :])
                    last.then_inc(blk_turned, 1)

                def product(to, at, col, n):
                    for part, q in enumerate((0, 0, 1)):
                        last = mm(to, ht[:, at.slot, q * P:(q + 1) * P], w_parts[:, part, col:col + n],
                                  start=part == 0, stop=part == 2)
                    return last

                def products(at):
                    pe.wait_ge(ht_kept, done(k * NB + at.g))
                    if k == 1:
                        pe.wait_ge(self_added, done(at.g - 1))
                        product(p_sum[:, 0:D], at, WCOLS - D, D).then_inc(self_made, 1)
                    for c in range(PER[k]):
                        pe.wait_ge(chunk_kept[c], CB[k][c] + at.g + 3 - BANKS[k])
                        product(pbig[:, bank(k, at, c), :], at, first_col_of + c * 512, 512).then_inc(chunk_made[c], 1)

                run_pass(pe, [(1, turn_blocks), (0, products)], count=NB, ring=2)

            pe.wait_ge(blocks_ready, 1)
            work(p_edge)
            for k in range(2):
                pe.wait_ge(units_made, k + 1)
                work(p_agnn[k])
            pe.wait_ge(weights_split, 1)
            build(0)
            work(p_plain[0])
            build(1)
            work(p_plain[1])


def kernel(x, src, dst, edge_type_16, edge_type_32, edge_weight, L1_gnn_beta, L2_gnn_weight,
           L3_gnn_basis, L3_gnn_coeff, L3_gnn_self_weight, L3_gnn_bias):
    import numpy as np
    import concourse.bacc as bacc
    from concourse.bass_utils import run_bass_kernel_spmd

    given = dict(x=x, src=src, dst=dst, type_a=edge_type_16, type_b=edge_type_32, weight=edge_weight,
                 beta=L1_gnn_beta, w_a=L2_gnn_weight, basis=L3_gnn_basis, coeff=L3_gnn_coeff,
                 w_self=L3_gnn_self_weight, bias=L3_gnn_bias)
    nc = bacc.Bacc("TRN2", target_bir_lowering=False, num_devices=1)
    arrays, args = {}, []
    for name, a in given.items():
        a = np.ascontiguousarray(a)
        arrays[f"in_{name}"] = a
        args.append(nc.dram_tensor(f"in_{name}", a.shape, mybir.dt.from_np(a.dtype), kind="ExternalInput").ap())
    out = nc.dram_tensor("out", np.shape(x), F32, kind="ExternalOutput").ap()
    gnn_program(nc, *args, out)
    r = run_bass_kernel_spmd(nc, [arrays], core_ids=[0])
    return r.results[0]["out"]
```
